# Optimizing a Trainium2 kernel written in Bass

```python
import numpy as np
import jax
import jax.numpy as jnp

def _softmax(x, axis=-1):
    return jax.nn.softmax(x, axis=axis)
def _gelu(x):
    return jax.nn.gelu(x, approximate=True)
def _silu(x):
    return jax.nn.silu(x)
def _sigmoid(x):
    return jax.nn.sigmoid(x)
def _layernorm(x, axis=-1, eps=1e-5):
    m = jnp.mean(x, axis=axis, keepdims=True)
    v = jnp.var(x, axis=axis, keepdims=True)
    return (x - m) / jnp.sqrt(v + eps)
def _scatter_add(tgt, idx, src, axis=0):
    return tgt.at[idx].add(src)
def _segment_sum(src, seg, n):
    return jax.ops.segment_sum(src, seg, n)

kernel_name = 'mk_metaformer_d2_conv_nchw128_13fca7'

def setup_inputs(seed: int = 0):
    np.random.seed(seed)
    _w = jnp.asarray
    def _rec_inputs():
        import jax
        import jax.numpy as jnp
        _gk = jax.random.key(seed)
        x = -0.0005207 + 1.001 * jax.random.normal(jax.random.fold_in(_gk, 1), (4, 128, 64, 64), jnp.float32)
        return x
    x = _rec_inputs()
    def _L0_conv_setup():
        import jax, jax.numpy as jnp
        import numpy as np
        K = 7
        DIL = 2
        PAD = 6
        G = 8
        key = jax.random.key(seed)
        ks = jax.random.split(key, 5)
        B, C, H, W = (4, 128, 64, 64)
        Cr = C // 4
        KKG = K * K * G
        return {'x': jax.random.normal(ks[0], (B, C, H, W), jnp.float32), 'w_reduce': jax.random.normal(ks[1], (Cr, C), jnp.float32) * 0.05, 'b_reduce': jax.random.normal(ks[2], (Cr,), jnp.float32) * 0.05, 'w_span': jax.random.normal(ks[3], (KKG, Cr), jnp.float32) * 0.05, 'b_span': jax.random.normal(ks[4], (KKG,), jnp.float32) * 0.05}
    _L0_conv_all = _L0_conv_setup()
    _L0_conv_in = {k: v for k, v in _L0_conv_all.items() if k in ('w_reduce', 'b_reduce', 'w_span', 'b_span', )}
    del _L0_conv_all

    def _L0_ffn_setup():
        import jax, jax.numpy as jnp
        import numpy as np
        PADDED_SL = 8192
        TEMPERATURE = 1.0
        SIGMA_POW = 0.25

        def _stu_conv(phi, u, n):
            b, sl, d = u.shape
            sgn = jnp.where(jnp.arange(sl) % 2 == 0, 1.0, -1.0).astype(u.dtype)
            sgn3 = sgn[None, :, None]
            Vf = jnp.fft.rfft(phi, n=n, axis=0)
            Uf_p = jnp.fft.rfft(u, n=n, axis=1)
            Uf_m = jnp.fft.rfft(u * sgn3, n=n, axis=1)
            U_plus = jnp.fft.irfft(Vf[None, :, :, None] * Uf_p[:, :, None, :], n=n, axis=1)[:, :sl]
            U_minus = jnp.fft.irfft(Vf[None, :, :, None] * Uf_m[:, :, None, :], n=n, axis=1)[:, :sl]
            U_minus = U_minus * sgn[None, :, None, None]
            return (U_plus, U_minus)

        def _compute_spectral(u, sigma, phi, Mpp, Mpm):
            U_plus, U_minus = _stu_conv(phi, u, PADDED_SL)
            s = sigma ** SIGMA_POW
            out = jnp.einsum('btkd,k,kde->bte', U_plus, s, Mpp)
            out = out + jnp.einsum('btkd,k,kde->bte', U_minus, s, Mpm)
            return out

        def _compute_ar_u(Mu, u):
            sl = u.shape[1]
            out = jnp.zeros(u.shape[:2] + (Mu.shape[-1],), dtype=u.dtype)
            for i in range(Mu.shape[0]):
                ui = jnp.pad(u, ((0, 0), (i, 0), (0, 0)))[:, :sl]
                out = out + jnp.einsum('btd,de->bte', ui, Mu[i])
            return out

        def _stu(u, sigma, phi, Mu, Mpp, Mpm):
            return _compute_spectral(u, sigma, phi, Mpp, Mpm) + _compute_ar_u(Mu, u)
        key = jax.random.key(seed)
        ks = jax.random.split(key, 8)
        b, sl, d, K, k_u = (2, 4096, 128, 16, 3)
        x = jax.random.normal(ks[0], (b, sl, d), dtype=jnp.float32)
        sigma = jax.random.uniform(ks[1], (K,), dtype=jnp.float32, minval=0.001, maxval=1.0)
        phi = jax.random.normal(ks[2], (sl, K), dtype=jnp.float32) / np.sqrt(sl)
        M_u = jax.random.normal(ks[3], (4, k_u, d, d), dtype=jnp.float32) * 0.02
        M_phi_plus = jax.random.normal(ks[4], (4, K, d, d), dtype=jnp.float32) * 0.02
        M_phi_minus = jax.random.normal(ks[5], (4, K, d, d), dtype=jnp.float32) * 0.02
        log_weights = jnp.ones((4,), dtype=jnp.float32)
        u01 = jax.random.uniform(ks[6], (4,), dtype=jnp.float32, minval=1e-06, maxval=1.0 - 1e-06)
        gumbel = -jnp.log(-jnp.log(u01))
        return {'x': x, 'sigma': sigma, 'phi': phi, 'M_u': M_u, 'M_phi_plus': M_phi_plus, 'M_phi_minus': M_phi_minus, 'log_weights': log_weights, 'gumbel': gumbel}
    _L0_ffn_all = _L0_ffn_setup()
    _L0_ffn_in = {k: v for k, v in _L0_ffn_all.items() if k in ('sigma', 'phi', 'M_u', 'M_phi_plus', 'M_phi_minus', 'log_weights', 'gumbel', )}
    del _L0_ffn_all

    def _L1_conv_setup():
        import jax, jax.numpy as jnp
        import numpy as np
        N, C_IN, C_OUT, H, W = (64, 128, 128, 64, 64)
        K, RED = (3, 16)
        key = jax.random.key(seed)
        ks = jax.random.split(key, 12)
        s = 0.02
        return {'x': jax.random.normal(ks[0], (N, C_IN, H, W), dtype=jnp.float32), 'W_sp': jax.random.normal(ks[1], (16, K * K), dtype=jnp.float32) * s, 'b_sp': jnp.zeros((K * K,), dtype=jnp.float32), 'W_o1': jax.random.normal(ks[2], (C_IN, C_OUT // RED), dtype=jnp.float32) * s, 'b_o1': jnp.zeros((C_OUT // RED,), dtype=jnp.float32), 'W_o2': jax.random.normal(ks[3], (C_OUT // RED, C_OUT), dtype=jnp.float32) * s, 'b_o2': jnp.zeros((C_OUT,), dtype=jnp.float32), 'W_i1': jax.random.normal(ks[4], (C_IN, C_IN // RED), dtype=jnp.float32) * s, 'b_i1': jnp.zeros((C_IN // RED,), dtype=jnp.float32), 'W_i2': jax.random.normal(ks[5], (C_IN // RED, C_IN), dtype=jnp.float32) * s, 'b_i2': jnp.zeros((C_IN,), dtype=jnp.float32)}
    _L1_conv_all = _L1_conv_setup()
    _L1_conv_in = {k: v for k, v in _L1_conv_all.items() if k in ('W_sp', 'b_sp', 'W_o1', 'b_o1', 'W_o2', 'b_o2', 'W_i1', 'b_i1', 'W_i2', 'b_i2', )}
    del _L1_conv_all

    def _L1_ffn_setup():
        import jax, jax.numpy as jnp
        import numpy as np
        B, N, D, C, E, K = (8, 8192, 128, 128, 8, 2)
        key = jax.random.key(seed)
        k0, k1, k2 = jax.random.split(key, 3)
        x = jax.random.normal(k0, (B, N, D), dtype=jnp.float32)
        router_w = jax.random.normal(k1, (D, E), dtype=jnp.float32) * 0.05
        router_b = jnp.zeros((E,), dtype=jnp.float32)
        expert_w = jax.random.normal(k2, (E, D, C), dtype=jnp.float32) * (1.0 / np.sqrt(D))
        expert_b = jnp.zeros((E, C), dtype=jnp.float32)
        return {'x': x, 'router_w': router_w, 'router_b': router_b, 'expert_w': expert_w, 'expert_b': expert_b}
    _L1_ffn_all = _L1_ffn_setup()
    _L1_ffn_in = {k: v for k, v in _L1_ffn_all.items() if k in ('router_w', 'router_b', 'expert_w', 'expert_b', )}
    del _L1_ffn_all

    return {
        "x": x,
        "L0_conv_w_reduce": _L0_conv_in["w_reduce"],
        "L0_conv_b_reduce": _L0_conv_in["b_reduce"],
        "L0_conv_w_span": _L0_conv_in["w_span"],
        "L0_conv_b_span": _L0_conv_in["b_span"],
        "L0_ffn_sigma": _L0_ffn_in["sigma"],
        "L0_ffn_phi": _L0_ffn_in["phi"],
        "L0_ffn_M_u": _L0_ffn_in["M_u"],
        "L0_ffn_M_phi_plus": _L0_ffn_in["M_phi_plus"],
        "L0_ffn_M_phi_minus": _L0_ffn_in["M_phi_minus"],
        "L0_ffn_log_weights": _L0_ffn_in["log_weights"],
        "L0_ffn_gumbel": _L0_ffn_in["gumbel"],
        "L1_conv_W_sp": _L1_conv_in["W_sp"],
        "L1_conv_b_sp": _L1_conv_in["b_sp"],
        "L1_conv_W_o1": _L1_conv_in["W_o1"],
        "L1_conv_b_o1": _L1_conv_in["b_o1"],
        "L1_conv_W_o2": _L1_conv_in["W_o2"],
        "L1_conv_b_o2": _L1_conv_in["b_o2"],
        "L1_conv_W_i1": _L1_conv_in["W_i1"],
        "L1_conv_b_i1": _L1_conv_in["b_i1"],
        "L1_conv_W_i2": _L1_conv_in["W_i2"],
        "L1_conv_b_i2": _L1_conv_in["b_i2"],
        "L1_ffn_router_w": _L1_ffn_in["router_w"],
        "L1_ffn_router_b": _L1_ffn_in["router_b"],
        "L1_ffn_expert_w": _L1_ffn_in["expert_w"],
        "L1_ffn_expert_b": _L1_ffn_in["expert_b"],
    }

def reference(x, L0_conv_w_reduce, L0_conv_b_reduce, L0_conv_w_span, L0_conv_b_span, L0_ffn_sigma, L0_ffn_phi, L0_ffn_M_u, L0_ffn_M_phi_plus, L0_ffn_M_phi_minus, L0_ffn_log_weights, L0_ffn_gumbel, L1_conv_W_sp, L1_conv_b_sp, L1_conv_W_o1, L1_conv_b_o1, L1_conv_W_o2, L1_conv_b_o2, L1_conv_W_i1, L1_conv_b_i1, L1_conv_W_i2, L1_conv_b_i2, L1_ffn_router_w, L1_ffn_router_b, L1_ffn_expert_w, L1_ffn_expert_b):
    import jax
    import jax.numpy as jnp
    def _L0_conv_ref(x, w_reduce, b_reduce, w_span, b_span):
        import jax, jax.numpy as jnp
        import numpy as np
        K = 7
        DIL = 2
        PAD = 6
        G = 8
        B, C, H, W = x.shape
        Cg = C // G
        red = jnp.einsum('bchw,oc->bohw', x, w_reduce) + b_reduce[None, :, None, None]
        ker = jnp.einsum('bohw,ko->bkhw', red, w_span) + b_span[None, :, None, None]
        ker = ker.reshape(B, G, K * K, H, W)
        xp = jnp.pad(x, ((0, 0), (0, 0), (PAD, PAD), (PAD, PAD)))
        patches = jnp.stack([xp[:, :, i * DIL:i * DIL + H, j * DIL:j * DIL + W] for i in range(K) for j in range(K)], axis=2)
        patches = patches.reshape(B, G, Cg, K * K, H, W)
        out = jnp.einsum('bgckhw,bgkhw->bgchw', patches, ker)
        return out.reshape(B, C, H, W)

    def _L0_ffn_ref(x, sigma, phi, M_u, M_phi_plus, M_phi_minus, log_weights, gumbel):
        import jax, jax.numpy as jnp
        import numpy as np
        PADDED_SL = 8192
        TEMPERATURE = 1.0
        SIGMA_POW = 0.25

        def _stu_conv(phi, u, n):
            b, sl, d = u.shape
            sgn = jnp.where(jnp.arange(sl) % 2 == 0, 1.0, -1.0).astype(u.dtype)
            sgn3 = sgn[None, :, None]
            Vf = jnp.fft.rfft(phi, n=n, axis=0)
            Uf_p = jnp.fft.rfft(u, n=n, axis=1)
            Uf_m = jnp.fft.rfft(u * sgn3, n=n, axis=1)
            U_plus = jnp.fft.irfft(Vf[None, :, :, None] * Uf_p[:, :, None, :], n=n, axis=1)[:, :sl]
            U_minus = jnp.fft.irfft(Vf[None, :, :, None] * Uf_m[:, :, None, :], n=n, axis=1)[:, :sl]
            U_minus = U_minus * sgn[None, :, None, None]
            return (U_plus, U_minus)

        def _compute_spectral(u, sigma, phi, Mpp, Mpm):
            U_plus, U_minus = _stu_conv(phi, u, PADDED_SL)
            s = sigma ** SIGMA_POW
            out = jnp.einsum('btkd,k,kde->bte', U_plus, s, Mpp)
            out = out + jnp.einsum('btkd,k,kde->bte', U_minus, s, Mpm)
            return out

        def _compute_ar_u(Mu, u):
            sl = u.shape[1]
            out = jnp.zeros(u.shape[:2] + (Mu.shape[-1],), dtype=u.dtype)
            for i in range(Mu.shape[0]):
                ui = jnp.pad(u, ((0, 0), (i, 0), (0, 0)))[:, :sl]
                out = out + jnp.einsum('btd,de->bte', ui, Mu[i])
            return out

        def _stu(u, sigma, phi, Mu, Mpp, Mpm):
            return _compute_spectral(u, sigma, phi, Mpp, Mpm) + _compute_ar_u(Mu, u)
        T = x.shape[1]
        outs = []
        for i, frac in enumerate((1, 2, 4, 8)):
            xi = x[:, :T // frac]
            si = _stu(xi, sigma, phi, M_u[i], M_phi_plus[i], M_phi_minus[i])
            si = jnp.pad(si, ((0, 0), (0, T - si.shape[1]), (0, 0)))
            outs.append(si)
        y_soft = jax.nn.softmax((log_weights + gumbel) / TEMPERATURE)
        y_hard = jax.nn.one_hot(jnp.argmax(y_soft), 4, dtype=y_soft.dtype)
        weights = y_hard - jax.lax.stop_gradient(y_soft) + y_soft
        stacked = jnp.stack(outs, axis=-1)
        return jnp.sum(stacked * weights, axis=-1)

    def _L1_conv_ref(x, W_sp, b_sp, W_o1, b_o1, W_o2, b_o2, W_i1, b_i1, W_i2, b_i2):
        import jax, jax.numpy as jnp
        import numpy as np
        N, C_IN, C_OUT, H, W = (64, 128, 128, 64, 64)
        K, RED = (3, 16)
        n, c, h, w = x.shape
        xs = x.reshape(n, c, 4, h // 4, 4, w // 4).mean(axis=(3, 5))
        xs = xs.reshape(n, c, 16).mean(axis=1)
        sp = (xs @ W_sp + b_sp).reshape(n, K, K)
        gap = x.mean(axis=(2, 3))
        co = jax.nn.relu(gap @ W_o1 + b_o1) @ W_o2 + b_o2
        ci = jax.nn.relu(gap @ W_i1 + b_i1) @ W_i2 + b_i2
        weight = co[:, :, None, None, None] * ci[:, None, :, None, None] * sp[:, None, None, :, :]

        def per_sample_conv(xi, wi):
            return jax.lax.conv_general_dilated(xi[None], wi, window_strides=(1, 1), padding=[(1, 1), (1, 1)])[0]
        return jax.vmap(per_sample_conv)(x, weight)

    def _L1_ffn_ref(x, router_w, router_b, expert_w, expert_b):
        import jax, jax.numpy as jnp
        import numpy as np
        B, N, D, C, E, K = (8, 8192, 128, 128, 8, 2)
        router_probs = jax.nn.softmax(x @ router_w + router_b, axis=-1)
        top_p, top_i = jax.lax.top_k(router_probs, K)
        top_p = top_p / jnp.sum(top_p, axis=-1, keepdims=True)
        expert_out = jnp.einsum('bnd,edc->bnec', x, expert_w) + expert_b
        gathered = jnp.take_along_axis(expert_out, top_i[..., None], axis=2)
        return jnp.einsum('bnk,bnkc->bnc', top_p, gathered)

    def _gn(v, G=32, eps=1e-5):
        B_, C_, H_, W_ = v.shape
        g = v.reshape(B_, G, C_ // G, H_, W_)
        m = jnp.mean(g, axis=(2, 3, 4), keepdims=True)
        s = jnp.var(g, axis=(2, 3, 4), keepdims=True)
        return ((g - m) / jnp.sqrt(s + eps)).reshape(v.shape)

    def _ln_c(v, eps=1e-6):
        m = jnp.mean(v, axis=1, keepdims=True)
        s = jnp.var(v, axis=1, keepdims=True)
        return (v - m) / jnp.sqrt(s + eps)

    def _ln_t(v, eps=1e-5):
        m = jnp.mean(v, axis=-1, keepdims=True)
        s = jnp.var(v, axis=-1, keepdims=True)
        return (v - m) / jnp.sqrt(s + eps)

    def _to_tokens(v):
        B_, C_, H_, W_ = v.shape
        return v.reshape(B_, C_, H_ * W_).transpose(0, 2, 1)
    def _from_tokens(t, like):
        B_, C_, H_, W_ = like.shape
        return t.transpose(0, 2, 1).reshape(B_, C_, H_, W_)

    x = x + _L0_conv_ref(_ln_c(x), L0_conv_w_reduce, L0_conv_b_reduce, L0_conv_w_span, L0_conv_b_span)
    t = _to_tokens(x)
    t = t + _L0_ffn_ref(_ln_t(t), L0_ffn_sigma, L0_ffn_phi, L0_ffn_M_u, L0_ffn_M_phi_plus, L0_ffn_M_phi_minus, L0_ffn_log_weights, L0_ffn_gumbel)
    x = _from_tokens(t, x)
    x = x + _L1_conv_ref(_ln_c(x), L1_conv_W_sp, L1_conv_b_sp, L1_conv_W_o1, L1_conv_b_o1, L1_conv_W_o2, L1_conv_b_o2, L1_conv_W_i1, L1_conv_b_i1, L1_conv_W_i2, L1_conv_b_i2)
    t = _to_tokens(x)
    t = t + _L1_ffn_ref(_ln_t(t), L1_ffn_router_w, L1_ffn_router_b, L1_ffn_expert_w, L1_ffn_expert_b)
    x = _from_tokens(t, x)
    return x


_drawn_inputs = setup_inputs


def setup_inputs(seed=0):
    import zlib

    import numpy as np

    out = dict(_drawn_inputs(seed))
    spreads = {'L0_ffn_log_weights': (1.0, 0.2),
     'L1_conv_b_sp': (0.0, 0.1),
     'L1_conv_b_o1': (0.0, 0.8),
     'L1_conv_b_o2': (0.0, 0.1),
     'L1_conv_b_i1': (0.0, 0.737),
     'L1_conv_b_i2': (0.0, 0.1),
     'L1_ffn_router_b': (0.0, 0.1),
     'L1_ffn_expert_b': (0.0, 0.1)}
    factors = {'L1_conv_W_o1': 31.195, 'L1_conv_W_o2': 8.0, 'L1_conv_W_i1': 33.908, 'L1_conv_W_i2': 7.026}
    for name, (base, spread) in spreads.items():
        noise = np.random.default_rng([zlib.crc32(name.encode()), seed]).standard_normal(out[name].shape)
        drawn = base * np.exp(spread * noise) if base else spread * noise
        out[name] = jnp.asarray(drawn.astype(out[name].dtype))
    for name, factor in factors.items():
        out[name] = (out[name] * factor).astype(out[name].dtype)
    return out
```

```python
from contextlib import ExitStack

import numpy as np
import concourse.bass as bass
from concourse import mybir

F32 = mybir.dt.float32
BF16 = mybir.dt.bfloat16
ALU = mybir.AluOpType
ACT = mybir.ActivationFunctionType
AX = mybir.AxisListType

NB, C, H, W = 4, 128, 64, 64
T = H * W
P = 128
CH = 512
NCH = T // CH
NT = CH // P
KW, DIL, PADW, NG = 7, 2, 6, 8
TAPS = KW * KW
CG = C // NG
WP = W + 2 * PADW
RT = T // P
SLOTS = RT + KW - 1
NE = 8
KF = 16
KX = KF + 2
NF1, NF2, NA = 17, 128, 16
FT = 32
EPS_C, EPS_T = 1e-6, 1e-5


class Arena:

    def __init__(self, nc, tag):
        self.nc, self.tag, self.ctx = nc, tag, ExitStack()

    def __enter__(self):
        return self

    def __exit__(self, *a):
        return self.ctx.__exit__(*a)

    def sb(self, name, shape, dt=F32):
        return self.ctx.enter_context(self.nc.sbuf_tensor(f"{self.tag}_{name}", shape, dt))

    def ps(self, name, shape, dt=F32):
        return self.ctx.enter_context(self.nc.psum_tensor(f"{self.tag}_{name}", shape, dt))

    def sem(self, name):
        return self.ctx.enter_context(self.nc.semaphore(f"{self.tag}_{name}"))


def split3(eng, src, tmp, hi, mid, lo, step):
    step(eng.tensor_copy(hi, src))
    step(eng.tensor_tensor(tmp, src, hi, ALU.subtract))
    step(eng.tensor_copy(mid, tmp))
    step(eng.tensor_tensor(lo, tmp, mid, ALU.subtract))


def prepare(nc, I, S):
    with Arena(nc, "prep") as A:
        lg = A.sb("lg", [P, 2, 4])
        sm = A.sb("sm", [P, 12, 4])
        s1 = A.sb("s1", [P, 8])
        prio = A.sb("prio", [P, 4])
        sg = A.sb("sg", [P, 3, KF])
        wr = A.sb("wr", [32, C])
        br = A.sb("br", [32, 1])
        ws = A.sb("ws", [32, TAPS * NG])
        bs = A.sb("bs", [1, TAPS * NG])
        wc = A.sb("wc", [P, TAPS * NG])
        kb = A.sb("kb", [1, TAPS * NG])
        mp = A.sb("mp", [P, 2, KF * C])
        mu = A.sb("mu", [P, 3, C])
        acc = A.sb("acc", [P, 2, KF * C])
        au = A.sb("au", [P, 3, C])
        ab = A.sb("ab", [P, KX * C])
        tmp = A.sb("tmp", [P, KX * C])
        parts = A.sb("parts", [P, 3, KX * C], BF16)
        zero = A.sb("zero", [P, 2048])
        d2 = A.sb("d2", [P, 16, 4])
        mk = A.sb("mk", [P, 16])
        pw = A.ps("pw", [P, 512])
        pb = A.ps("pb", [1, 512])
        small_in = A.sem("small_in")
        mats_in = A.sem("mats_in")
        mats_used = A.sem("mats_used")
        wprod = A.sem("wprod")
        dve_done = A.sem("dve_done")
        act_done = A.sem("act_done")
        act_req = A.sem("act_req")
        wc_ready = A.sem("wc_ready")
        parts_ready = A.sem("parts_ready")
        parts_out = A.sem("parts_out")
        zero_ready = A.sem("zero_ready")
        out_done = A.sem("out_done")
        block = A.ctx.enter_context(nc.Block())

        @block.sync
        def _(sp):
            sp.dma_start(lg[:, 0, :], I["lw"].partition_broadcast(P)).then_inc(small_in, 16)
            sp.dma_start(lg[:, 1, :], I["gum"].partition_broadcast(P)).then_inc(small_in, 16)
            sp.dma_start(sg[:, 0, :], I["sigma"].partition_broadcast(P)).then_inc(small_in, 16)
            sp.dma_start(wr[:], I["w_reduce"]).then_inc(small_in, 16)
            sp.dma_start(br[:], I["b_reduce"]).then_inc(small_in, 16)
            sp.dma_start(ws[:], I["w_span"]).then_inc(small_in, 16)
            sp.dma_start(bs[:], I["b_span"]).then_inc(small_in, 16)
            sp.dma_start(prio[:], I["prio"]).then_inc(small_in, 16)
            sp.dma_start(d2[:], I["d2"].rearrange("p (a b) -> p a b", a=16)).then_inc(small_in, 16)
            for i in range(4):
                if i:
                    sp.wait_ge(mats_used, i)
                sp.dma_start(mp[:, 0, :].rearrange("d (k e) -> d k e", k=KF),
                             I["Mpp"][i].rearrange("k d e -> d k e")).then_inc(mats_in, 16)
                sp.dma_start(mp[:, 1, :].rearrange("d (k e) -> d k e", k=KF),
                             I["Mpm"][i].rearrange("k d e -> d k e")).then_inc(mats_in, 16)
                sp.dma_start(mu[:], I["Mu"][i].rearrange("k d e -> d k e")).then_inc(mats_in, 16)
            sp.wait_ge(zero_ready, 1)
            n = 0
            for b in range(NB):
                for side in (0, WP - PADW):
                    sp.dma_start(S["XN"][b][:, side:side + PADW, :], zero[0:H, 0:PADW * C].rearrange(
                        "h (w c) -> h w c", c=C)).then_inc(out_done, 16)
                    n += 1
            for b in range(NB):
                sp.dma_start(S["SF"][b, 32], zero[:, 0:256]).then_inc(out_done, 16)
                n += 1
            sp.dma_start(S["SP"][32], zero[:, 0:2 * KX]).then_inc(out_done, 16)
            sp.dma_start(S["VP"], zero[0:66, 0:NB * 66].rearrange("h (b w) -> h b w", b=NB)).then_inc(out_done, 16)
            sp.wait_ge(wc_ready, 3)
            sp.dma_start(S["WC"], wc[:]).then_inc(out_done, 16)
            sp.dma_start(S["KB"], kb[:]).then_inc(out_done, 16)
            sp.dma_start(S["D2M"], d2[:].rearrange("p a b -> p (a b)")).then_inc(out_done, 16)
            n += 5
            for x in range(2):
                sp.wait_ge(parts_ready, x + 1)
                for s in range(3):
                    sp.dma_start(S["AS"][x, s].rearrange("k d e -> d k e"), parts[:, s, :].rearrange(
                        "d (k e) -> d k e", k=KX)).then_inc(parts_out, 16)
            sp.wait_ge(parts_out, 96)
            sp.wait_ge(out_done, 16 * n)

        @block.tensor
        def _(pe):
            pe.wait_ge(small_in, 16 * 9)
            pe.matmul(pw[:, 0:TAPS * NG], wr[:], ws[:], start=True, stop=True).then_inc(wprod, 1)
            pe.matmul(pb[:, 0:TAPS * NG], br[:], ws[:], start=True, stop=True).then_inc(wprod, 1)

        @block.scalar
        def _(act):
            act.wait_ge(act_req, 1)
            act.activation(sm[:, 1, :], sm[:, 0, :], ACT.Exp).then_inc(act_done, 1)
            act.activation(sg[:, 1, :], sg[:, 0, :], ACT.Sqrt).then_inc(act_done, 1)
            act.wait_ge(act_done, 2)
            act.activation(sg[:, 2, :], sg[:, 1, :], ACT.Sqrt).then_inc(act_done, 1)

        @block.vector
        def _(v):
            n = [0]

            def step(ins):
                n[0] += 1
                ins.then_inc(dve_done, 1)
                v.wait_ge(dve_done, n[0])

            v.memset(zero[:], 0.0).then_inc(zero_ready, 1)
            v.wait_ge(small_in, 16 * 9)
            v.wait_ge(wprod, 2)
            v.tensor_copy(wc[:], pw[:, 0:TAPS * NG]).then_inc(wc_ready, 1)
            v.tensor_tensor(kb[:], pb[:, 0:TAPS * NG], bs[:], ALU.add).then_inc(wc_ready, 1)
            step(v.tensor_tensor(sm[:, 2, :], lg[:, 0, :], lg[:, 1, :], ALU.add))
            step(v.tensor_reduce(s1[:, 0:1], sm[:, 2, :], AX.X, ALU.max))
            v.tensor_scalar(sm[:, 0, :], sm[:, 2, :], s1[:, 0:1], None, ALU.subtract).then_inc(act_req, 1)
            v.wait_ge(act_done, 3)
            step(v.tensor_reduce(s1[:, 1:2], sm[:, 1, :], AX.X, ALU.add))
            step(v.reciprocal(s1[:, 2:3], s1[:, 1:2]))
            step(v.tensor_scalar(sm[:, 3, :], sm[:, 1, :], s1[:, 2:3], None, ALU.mult))
            step(v.tensor_reduce(s1[:, 3:4], sm[:, 3, :], AX.X, ALU.max))
            step(v.tensor_scalar(sm[:, 4, :], sm[:, 3, :], s1[:, 3:4], None, ALU.is_equal))
            step(v.tensor_tensor(sm[:, 5, :], sm[:, 4, :], prio[:], ALU.mult))
            step(v.tensor_reduce(s1[:, 4:5], sm[:, 5, :], AX.X, ALU.max))
            step(v.tensor_scalar(sm[:, 6, :], sm[:, 5, :], s1[:, 4:5], None, ALU.is_equal))
            step(v.tensor_tensor(sm[:, 7, :], sm[:, 6, :], sm[:, 3, :], ALU.subtract))
            step(v.tensor_tensor(sm[:, 8, :], sm[:, 7, :], sm[:, 3, :], ALU.add))
            step(v.memset(mk[:], 0.0))
            for i in range(4):
                step(v.tensor_scalar(mk[:, 0:16 >> i], mk[:, 0:16 >> i], sm[:, 6, i:i + 1], None, ALU.add))
            v.tensor_tensor(d2[:], d2[:], mk[:].rearrange("p (a o) -> p a o", o=1).to_broadcast([P, 16, 4]),
                            ALU.mult).then_inc(wc_ready, 1)
            for i in range(4):
                v.wait_ge(mats_in, 48 * (i + 1))
                wi = sm[:, 8, i:i + 1]
                for dst, src in ((acc, mp), (au, mu)):
                    if i == 0:
                        last = v.tensor_scalar(dst[:], src[:], wi, None, ALU.mult)
                    else:
                        last = v.scalar_tensor_tensor(dst[:], src[:], wi, dst[:], ALU.mult, ALU.add)
                    step(last)
                v.sem_inc(mats_used, 1)
            sv = sg[:, 2, :].rearrange("p (k o) -> p k o", o=1).to_broadcast([P, KF, C])
            for x, (op, m) in enumerate(((ALU.add, 0), (ALU.subtract, 1))):
                step(v.tensor_tensor(tmp[:, 0:KF * C], acc[:, 0, :], acc[:, 1, :], op))
                step(v.tensor_tensor(ab[:, 0:KF * C].rearrange("p (k e) -> p k e", k=KF),
                                     tmp[:, 0:KF * C].rearrange("p (k e) -> p k e", k=KF), sv, ALU.mult))
                step(v.tensor_copy(ab[:, KF * C:KF * C + C], au[:, m, :]))
                step(v.tensor_copy(ab[:, KF * C + C:], au[:, 2, :]))
                if x:
                    v.wait_ge(parts_out, 48)
                split3(v, ab[:], tmp[:], parts[:, 0, :], parts[:, 1, :], parts[:, 2, :], step)
                v.sem_inc(parts_ready, 1)



def normalise_in(nc, I, S):
    NQ = NB * NCH
    with Arena(nc, "lnc") as A:
        ident = A.sb("ident", [P, P])
        eps = A.sb("eps", [P, 1])
        xc = A.sb("xc", [P, 2, CH])
        xt = A.sb("xt", [P, 2, NT, C])
        xn = A.sb("xn", [P, 2, NT, C])
        xnc = A.sb("xnc", [P, 2, CH])
        st = A.sb("st", [P, 2, NT, 6])
        mv = A.sb("mv", [P, 2, NT, 2])
        sd = A.sb("sd", [P, 2, NT])
        rs = A.sb("rs", [P, 2, NT])
        nm = A.sb("nm", [P, 2, NT])
        px = A.ps("px", [P, 2, CH])
        pn = A.ps("pn", [P, 2, CH])
        const_in = A.sem("const_in")
        x_in = [A.sem(f"x_in{k}") for k in range(2)]
        outs = [A.sem(f"outs{k}") for k in range(2)]
        x_turned, xt_ready, st_ready = A.sem("x_turned"), A.sem("xt_ready"), A.sem("st_ready")
        mv_ready, sd_ready, rs_ready = A.sem("mv_ready"), A.sem("sd_ready"), A.sem("rs_ready")
        nm_ready, xn_ready, xn_turned = A.sem("nm_ready"), A.sem("xn_ready"), A.sem("xn_turned")
        xnc_ready, eps_ready = A.sem("xnc_ready"), A.sem("eps_ready")
        passed = A.sem("passed")
        block = A.ctx.enter_context(nc.Block())
        xv = I["x"].rearrange("b c (n m) -> b n c m", m=CH)

        @block.gpsimd
        def _(pool):
            pool.memset(eps[:], EPS_C).then_inc(eps_ready, 1)
            with pool.Fori(0, NQ // 2) as i:
                for k in range(2):
                    q = 2 * i + k
                    pool.wait_ge(x_turned, q + 1)
                    pool.dma_start(xc[:, k, :], xv[bass.ds(q // NCH, 1), bass.ds(q % NCH, 1)].rearrange(
                        "o a c m -> (o a c) m")).then_inc(x_in[k], 16)

        @block.sync
        def _(sp):
            sp.dma_start(ident[:], I["ident"]).then_inc(const_in, 16)
            rows = S["XN"].rearrange("b (n t r) w c -> b n r w t c", t=NT, r=2)
            with sp.Fori(0, NQ // 2) as i:
                for k in range(2):
                    q = 2 * i + k
                    sp.wait_ge(xn_ready, q + 1)
                    sp.dma_start(S["XT"].rearrange("(q t p) c -> q p t c", p=P, t=NT)[bass.ds(q, 1)].rearrange(
                        "o p t c -> (o p) t c"), xt[:, k]).then_inc(outs[k], 16)
                    for r in range(2):
                        sp.dma_start(rows[bass.ds(q // NCH, 1), bass.ds(q % NCH, 1), r, PADW:PADW + W].rearrange(
                            "o a w t c -> (o a w) t c"), xn[64 * r:64 * r + 64, k]).then_inc(outs[k], 16)
                    sp.wait_ge(xnc_ready, q + 3)
                    sp.dma_start(S["XNC"][bass.ds(q, 1)].rearrange("o c m -> (o c) m"),
                                 xnc[:, k]).then_inc(outs[k], 16)
            for k in range(2):
                sp.wait_ge(outs[k], 64 * (NQ // 2) + 64)

        @block.tensor
        def _(pe):
            pe.wait_ge(const_in, 16)
            with pe.Fori(0, NQ // 2) as i:
                for k in range(2):
                    pe.wait_ge(x_in[k], 16 * i + 16)
                    pe.wait_ge(xt_ready, 2 * i + k + 1)
                    for t in range(NT):
                        m = pe.transpose(px[:, k, t * P:(t + 1) * P], xc[:, k, t * P:(t + 1) * P], ident[:])
                    m.then_inc(x_turned, 1)
                for k in range(2):
                    pe.wait_ge(xn_ready, 2 * i + k + 1)
                    pe.wait_ge(xnc_ready, 2 * i + k + 1)
                    for t in range(NT):
                        m = pe.transpose(pn[:, k, t * P:(t + 1) * P], xn[:, k, t, :], ident[:])
                    m.then_inc(xn_turned, 1)

        @block.scalar
        def _(act):
            act.sem_inc(x_turned, 2)
            act.sem_inc(xt_ready, 2)
            act.sem_inc(xnc_ready, 2)
            for k in range(2):
                act.sem_inc(outs[k], 64)
            act.wait_ge(eps_ready, 1)
            with act.Fori(0, NQ // 2) as i:
                for k in range(2):
                    act.wait_ge(x_turned, 2 * i + k + 3)
                    act.wait_ge(outs[k], 64 * i + 64)
                    act.activation(xt[:, k], px[:, k].rearrange("p (t c) -> p t c", t=NT), ACT.Copy).then_inc(xt_ready, 1)
                for k in range(2):
                    act.wait_ge(mv_ready, 2 * i + k + 1)
                    act.activation(sd[:, k], mv[:, k, :, 1], ACT.Sqrt, bias=eps[:]).then_inc(sd_ready, 1)
                for k in range(2):
                    act.wait_ge(nm_ready, 2 * i + k + 1)
                    act.wait_ge(xt_ready, 2 * i + k + 3)
                    for t in range(NT):
                        m = act.activation(xn[:, k, t, :], xt[:, k, t, :], ACT.Identity,
                                           bias=nm[:, k, t:t + 1], scale=rs[:, k, t:t + 1])
                    m.then_inc(xn_ready, 1)
                for k in range(2):
                    act.wait_ge(xn_turned, 2 * i + k + 1)
                    act.activation(xnc[:, k], pn[:, k], ACT.Copy).then_inc(xnc_ready, 1)

        @block.vector
        def _(v):
            with v.Fori(0, NQ // 2) as i:
                for k in range(2):
                    v.wait_ge(xt_ready, 2 * i + k + 3)
                    for t in range(NT):
                        m = v.bn_stats(st[:, k, t, :], xt[:, k, t, :])
                    m.then_inc(st_ready, 1)
                for k in range(2):
                    v.wait_ge(st_ready, 2 * i + k + 1)
                    v.sem_inc(passed, 1)
                    for t in range(NT):
                        m = v.bn_aggr(mv[:, k, t, :], st[:, k, t, :])
                    m.then_inc(mv_ready, 1)
                for k in range(2):
                    v.wait_ge(sd_ready, 2 * i + k + 1)
                    v.reciprocal(rs[:, k], sd[:, k]).then_inc(rs_ready, 1)
                for k in range(2):
                    v.wait_ge(rs_ready, 2 * i + k + 1)
                    v.scalar_tensor_tensor(nm[:, k], mv[:, k, :, 0], -1.0, rs[:, k],
                                           ALU.mult, ALU.mult).then_inc(nm_ready, 1)


NSING, NPAIR = 9, 20
ITEMS = ["s", "p", "p"] * NSING + ["p", "p"]
PR = 14
SR = 4
HT = 25


def involution(nc, I, S):
    items, t = [], 0
    for it in ITEMS:
        items.append((t,) if it == "s" else (t, t + 1))
        t += len(items[-1])
    assert t == TAPS
    pairs = [k for k, tt in enumerate(items) if len(tt) == 2]
    NI, NQ = len(items), NB * NCH
    pe_upto = [1 + max(k for k, tt in enumerate(items) if len(tt) == 1 and tt[0] < 7 * (g + 1)) for g in range(7)]
    pool_upto = [sum(items[k][0] < 7 * (g + 1) for k in pairs) for g in range(7)]
    M0 = TAPS * 8
    with Arena(nc, "inv") as A:
        ident = A.sb("ident", [P, P])
        wc = A.sb("wc", [P, TAPS * NG])
        kb = A.sb("kb", [1, TAPS * NG])
        ones = A.sb("ones", [1, P])
        xnc = A.sb("xnc", [P, 2, CH])
        X7 = A.sb("X7", [P, KW, SLOTS * C])
        prod = A.sb("prod", [P, PR, CH])
        psm = A.sb("psm", [P, SR, CH])
        cv = A.sb("cv", [P, 2, CH])
        ker = A.ps("ker", [P, 2, NT, 256])
        acc = A.ps("acc", [P, 2, CH])
        const_in, ones_ready, pads_ready = A.sem("const_in"), A.sem("ones_ready"), A.sem("pads_ready")
        xnc_in = [A.sem(f"xnc_in{k}") for k in range(2)]
        x7_in = [A.sem(f"x7_in{k}") for k in range(4)]
        ker_ready, mul_done, pair_done = A.sem("ker_ready"), A.sem("mul_done"), A.sem("pair_done")
        item_done, cv_ready = A.sem("item_done"), A.sem("cv_ready")
        cv_out = [A.sem(f"cv_out{k}") for k in range(2)]
        block = A.ctx.enter_context(nc.Block())
        G7 = 16 * 2 * KW

        def slot(c, tap):
            return 7 * ((7 * c + tap // 7) % 2) + tap % 7

        @block.sync
        def _(sp):
            for d, s in ((ident, I["ident"]), (wc, S["WC"]), (kb, S["KB"])):
                sp.dma_start(d[:], s).then_inc(const_in, 16)
            rows = S["XN"].rearrange("b (n t r) w c -> b n r w t c", t=NT, r=2)
            with sp.Fori(0, NQ // 4) as i:
                for c in range(4):
                    q = 4 * i + c
                    sp.wait_ge(mul_done, TAPS * (q + 2))
                    sp.wait_ge(x7_in[c], G7 * i + G7)
                    for j in range(KW):
                        for r in range(2):
                            dst = X7[64 * r:64 * r + 64, j, bass.ds((i % 2) * (16 * C) + (3 + 4 * c) * C, CH)]
                            sp.dma_start(dst.rearrange("p (t c) -> p t c", t=NT),
                                         rows[bass.ds(i // 2, 1), bass.ds((i % 2) * 4 + c, 1), r,
                                              DIL * j:DIL * j + W].rearrange("o a w t c -> (o a w) t c")
                                         ).then_inc(x7_in[c], 16)
            sp.wait_ge(x7_in[0], G7 * (NQ // 4) + G7)
            sp.sem_inc(x7_in[0], G7)

        @block.gpsimd
        def _(pool):
            for s0 in (0, SLOTS - 3):
                m = pool.memset(X7[:, :, s0 * C:(s0 + 3) * C], 0.0)
                m.then_inc(pads_ready, 1)
            pool.memset(ones[:], 1.0).then_inc(ones_ready, 1)
            pool.sem_inc(pair_done, NPAIR)
            with pool.Fori(0, NQ // 4) as i:
                for c in range(4):
                    q = 4 * i + c
                    for p, k in enumerate(pairs):
                        t0, t1 = items[k]
                        pool.wait_ge(mul_done, M0 + TAPS * q + t1 + 1)
                        old = pairs[p - SR]
                        pool.wait_ge(item_done, NI * q + old + 1 + (NI if p >= SR else 0))
                        pool.tensor_tensor(psm[:, p % SR, :], prod[:, slot(c, t0), :], prod[:, slot(c, t1), :],
                                           ALU.add).then_inc(pair_done, 1)

        @block.tensor
        def _(pe):
            pe.wait_ge(const_in, 48)
            pe.wait_ge(ones_ready, 1)

            def kernels(k, half):
                lo, hi = (0, HT * NG) if half == 0 else (HT * NG, TAPS * NG)
                for t in range(NT):
                    o = ker[:, half, t, 0:hi - lo]
                    pe.matmul(o, xnc[:, k, t * P:(t + 1) * P], wc[:, lo:hi], start=True, stop=False)
                    m = pe.matmul(o, ones[:], kb[:, lo:hi], start=False, stop=True)
                m.then_inc(ker_ready, 1)

            pe.wait_ge(xnc_in[0], 16)
            kernels(0, 0)
            with pe.Fori(0, NQ // 4) as i:
                for c in range(4):
                    q = 4 * i + c
                    pe.wait_ge(mul_done, M0 + TAPS * q)
                    kernels(c % 2, 1)
                    pe.wait_ge(cv_ready, q + 1)
                    for k, tt in enumerate(items):
                        if k == 16:
                            pe.wait_ge(mul_done, M0 + TAPS * q + HT)
                            pe.wait_ge(xnc_in[(c + 1) % 2], 16 * ((4 * i + c + 1) // 2) + 16)
                            kernels((c + 1) % 2, 0)
                        if len(tt) == 1:
                            pe.wait_ge(mul_done, M0 + TAPS * q + tt[0] + 1)
                            src = prod[:, slot(c, tt[0]), :]
                        else:
                            p = pairs.index(k)
                            pe.wait_ge(pair_done, NPAIR * q + NPAIR + p + 1)
                            src = psm[:, p % SR, :]
                        pe.matmul(acc[:, c % 2, :], ident[:], src, start=(k == 0),
                                  stop=(k == NI - 1)).then_inc(item_done, 1)

        @block.scalar
        def _(act):
            act.sem_inc(cv_ready, 2)
            act.sem_inc(item_done, NI)
            act.sem_inc(ker_ready, 1)
            for k in range(4):
                act.sem_inc(x7_in[k], G7)
            for k in range(2):
                act.sem_inc(cv_out[k], 16)

            def load(q, k):
                act.dma_start(xnc[:, k], q).then_inc(xnc_in[k], 16)

            xq = S["XNC"]
            load(xq[0], 0)
            load(xq[1], 1)
            with act.Fori(0, NQ // 4) as i:
                for c in range(4):
                    q, k = 4 * i + c, c % 2
                    act.wait_ge(ker_ready, 2 * q + 3)
                    load(xq[bass.ds((q + 2) % NQ, 1)].rearrange("o c m -> (o c) m"), k)
                    act.wait_ge(item_done, NI * q + 2 * NI)
                    act.wait_ge(cv_out[k], 16 * (2 * i + c // 2) + 16)
                    act.activation(cv[:, k], acc[:, k], ACT.Copy).then_inc(cv_ready, 1)
                    act.wait_ge(cv_ready, q + 3)
                    act.dma_start(S["CV"].rearrange("(q t p) c -> q p t c", p=P, t=NT)[bass.ds(q, 1)].rearrange(
                        "o p t c -> (o p) t c"), cv[:, k].rearrange("p (t c) -> p t c", t=NT)).then_inc(cv_out[k], 16)
            for k in range(2):
                act.wait_ge(cv_out[k], 16 * (NQ // 2) + 16)
                act.wait_ge(xnc_in[k], 16 * (NQ // 2 + 1))

        @block.vector
        def _(v):
            v.sem_inc(mul_done, M0)
            v.wait_ge(pads_ready, 2)
            with v.Fori(0, NQ // 4) as i:
                for c in range(4):
                    q = 4 * i + c
                    v.wait_ge(x7_in[c], G7 * i + 2 * G7)
                    if c < 3:
                        v.wait_ge(x7_in[c + 1], G7 * i + 2 * G7)
                    else:
                        v.wait_ge(x7_in[0], G7 * i + 3 * G7)
                    for tap in range(TAPS):
                        if tap % 7 == 0:
                            g = tap // 7
                            back = 0 if g >= 2 else 1
                            o = (g - 2) % 7
                            v.wait_ge(item_done, NI * q + pe_upto[o] + NI * (1 - back))
                            v.wait_ge(pair_done, NPAIR * q + pool_upto[o] + NPAIR * (1 - back))
                        if tap in (0, HT):
                            v.wait_ge(ker_ready, 2 * q + 2 + (tap > 0))
                        ti, tj = divmod(tap, KW)
                        h, w = (0, tap) if tap < HT else (1, tap - HT)
                        kv = ker[:, h, :, w * NG:(w + 1) * NG].rearrange("p t (g o) -> p t g o", o=1)
                        xv = X7[:, tj, bass.ds((i % 2) * (16 * C) + (4 * c + ti) * C, CH)]
                        v.tensor_tensor(prod[:, slot(c, tap), :].rearrange("p (t g c) -> p t g c", t=NT, g=NG),
                                        kv.to_broadcast([P, NT, NG, CG]),
                                        xv.rearrange("p (t g c) -> p t g c", t=NT, g=NG),
                                        ALU.mult).then_inc(mul_done, 1)


HH = 8


def forward(nc, I, S):
    NU = NB * 2
    with Arena(nc, "fwd") as A:
        ident = A.sb("ident", [P, P])
        d1 = A.sb("d1", [P, 2 * P])
        eps = A.sb("eps", [P, 1])
        xt = A.sb("xt", [P, 2, HH, 2, C])
        cv = A.sb("cv", [P, 2, HH, 2, C])
        u = A.sb("u", [P, 2, HH, 2, C])
        ph = A.sb("ph", [P, 16, 2 * KX])
        x1c = A.sb("x1c", [P, 2, T])
        so = A.sb("so", [P, 2, 2, HH, 2 * C])
        po = A.sb("po", [P, 2, 16, 2 * KX])
        st = A.sb("st", [P, 16, 6])
        mv = A.sb("mv", [P, 16, 2])
        sd = A.sb("sd", [P, 16])
        rs = A.sb("rs", [P, 16])
        nm = A.sb("nm", [P, 16])
        pt = A.ps("pt", [P, 4, CH])
        pf = A.ps("pf", [P, 4, CH])
        const_in, eps_ready = A.sem("const_in"), A.sem("eps_ready")
        x_in = [A.sem(f"x_in{k}") for k in range(2)]
        x1_ready, st_ready, mv_ready = A.sem("x1_ready"), A.sem("st_ready"), A.sem("mv_ready")
        sd_ready, rs_ready, nm_ready = A.sem("sd_ready"), A.sem("rs_ready"), A.sem("nm_ready")
        u_ready, turned, x1c_ready = A.sem("u_ready"), A.sem("turned"), A.sem("x1c_ready")
        f_done, so_ready = A.sem("f_done"), A.sem("so_ready")
        s_out = [A.sem(f"s_out{k}") for k in range(2)]
        c_out = A.sem("c_out")
        passed = A.sem("passed")
        block = A.ctx.enter_context(nc.Block())
        tok = "(b q k h p) c -> b k q (h p c)"

        @block.gpsimd
        def _(pool):
            pool.memset(eps[:], EPS_T).then_inc(eps_ready, 1)

        @block.sync
        def _(sp):
            sp.dma_start(ident[:], I["ident"]).then_inc(const_in, 16)
            sp.dma_start(d1[:], I["d1"]).then_inc(const_in, 16)
            sp.dma_start(ph[:], I["phix"].rearrange("(q h p) k -> q h (p k)", q=P, h=16)).then_inc(const_in, 16)
            with sp.Fori(0, NU // 2) as i:
                for k in range(2):
                    sp.wait_ge(turned, 4 * (2 * i + k) + 4)
                    sp.sem_inc(passed, 1)
                    sp.wait_ge(u_ready, 2 * i + k + 1)
                    for d, s in ((xt, "XT"), (cv, "CV")):
                        v = S[s].rearrange(tok, b=NB, q=P, k=2, h=HH)
                        sp.dma_start(d[:, k].rearrange("p i q c -> p (i q c)"), v[bass.ds(i, 1), k].rearrange(
                            "o q m -> (o q) m")).then_inc(x_in[k], 16)

        @block.vector
        def _(v):
            with v.Fori(0, NU // 2) as i:
                for k in range(2):
                    un = 2 * i + k
                    v.wait_ge(x_in[k], 32 * i + 32)
                    v.tensor_tensor(xt[:, k], xt[:, k], cv[:, k], ALU.add).then_inc(x1_ready, 1)
                    v.wait_ge(x1_ready, un + 1)
                    for t in range(16):
                        m = v.bn_stats(st[:, t, :], xt[:, k, t // 2, t % 2, :])
                    m.then_inc(st_ready, 1)
                    v.wait_ge(st_ready, un + 1)
                    v.wait_ge(sd_ready, un + 1)
                    v.sem_inc(passed, 1)
                    for t in range(16):
                        m = v.bn_aggr(mv[:, t, :], st[:, t, :])
                    m.then_inc(mv_ready, 1)
                    v.wait_ge(u_ready, un + 2)
                    v.wait_ge(sd_ready, un + 2)
                    v.reciprocal(rs[:], sd[:]).then_inc(rs_ready, 1)
                    v.wait_ge(rs_ready, un + 1)
                    v.scalar_tensor_tensor(nm[:], mv[:, :, 0], -1.0, rs[:], ALU.mult, ALU.mult).then_inc(nm_ready, 1)
                    v.wait_ge(s_out[1], 16 * un + 16)
                    for n in range(4):
                        v.wait_ge(f_done, 8 * un + 2 * n + 2)
                        v.tensor_copy(so[:, 1, k, 2 * n:2 * n + 2, :].rearrange("p h m -> p (h m)"),
                                      pf[:, 2 * (n % 2) + 1, :]).then_inc(so_ready, 1)
            for n in range(2):
                v.wait_ge(f_done, 8 * NU + 2 * n + 2)
                v.tensor_copy(po[:, 1, 8 * n:8 * n + 8, :].rearrange("p h m -> p (h m)"),
                              pf[:, 2 * n + 1, 0:16 * KX]).then_inc(so_ready, 1)

        so_a = A.sem("so_a")

        @block.scalar
        def _(act):
            act.sem_inc(turned, 4)
            act.sem_inc(x1c_ready, 4)
            act.sem_inc(u_ready, 2)
            act.sem_inc(sd_ready, 1)
            act.sem_inc(so_ready, 2)
            act.sem_inc(so_a, 2)
            act.sem_inc(s_out[0], 16)
            act.sem_inc(s_out[1], 16)
            act.sem_inc(c_out, 16)
            act.wait_ge(eps_ready, 1)
            with act.Fori(0, NU // 2) as i:
                for k in range(2):
                    un = 2 * i + k
                    act.wait_ge(mv_ready, un + 1)
                    act.activation(sd[:], mv[:, :, 1], ACT.Sqrt, bias=eps[:]).then_inc(sd_ready, 1)
                    if k == 0:
                        act.wait_ge(c_out, 16 * i + 16)
                    for n in range(4):
                        act.wait_ge(turned, 4 * un + n + 5)
                        dst = x1c[:, 0, :].rearrange("c (q m) -> c m q", q=P)[:, 16 * k + 4 * n:16 * k + 4 * n + 4]
                        act.activation(dst, pt[:, n, :].rearrange("c (m q) -> c m q", m=4),
                                       ACT.Copy).then_inc(x1c_ready, 1)
                    act.wait_ge(nm_ready, un + 1)
                    for t in range(16):
                        m = act.activation(u[:, k, t // 2, t % 2, :], xt[:, k, t // 2, t % 2, :], ACT.Identity,
                                           bias=nm[:, t:t + 1], scale=rs[:, t:t + 1])
                    m.then_inc(u_ready, 1)
                    act.wait_ge(s_out[0], 16 * un + 16)
                    for n in range(4):
                        act.wait_ge(f_done, 8 * un + 2 * n + 1)
                        act.activation(so[:, 0, k, 2 * n:2 * n + 2, :].rearrange("p h m -> p (h m)"),
                                       pf[:, 2 * (n % 2), :], ACT.Copy).then_inc(so_a, 1)
                    for half, ready, n0 in ((0, so_a, 2), (1, so_ready, 2)):
                        act.wait_ge(ready, 4 * un + 4 + n0)
                        dst = S["SF"][:, 16 * half:16 * half + 16].rearrange("b f (l y h) m -> b y (f l) (h m)", y=2, l=8)
                        act.dma_start(dst[bass.ds(i, 1), k].rearrange("o q m -> (o q) m"),
                                      so[:, half, k].rearrange("p h m -> p (h m)")).then_inc(s_out[half], 16)
                    if k == 1:
                        act.wait_ge(x1c_ready, 4 * un + 8)
                        act.dma_start(S["X1C"][bass.ds(i, 1)].rearrange("o c t -> (o c) t"),
                                      x1c[:, 0, :]).then_inc(c_out, 16)
            for n in range(2):
                act.wait_ge(f_done, 8 * NU + 2 * n + 1)
                act.activation(po[:, 0, 8 * n:8 * n + 8, :].rearrange("p h m -> p (h m)"),
                               pf[:, 2 * n, 0:16 * KX], ACT.Copy).then_inc(so_a, 1)
            for half, ready in ((0, so_a), (1, so_ready)):
                act.wait_ge(ready, 4 * NU + 4)
                act.dma_start(S["SP"][16 * half:16 * half + 16].rearrange("f (l h) m -> (f l) (h m)", l=8),
                              po[:, half].rearrange("p h m -> p (h m)")).then_inc(s_out[half], 16)
            act.wait_ge(c_out, 16 * NB + 16)
            for k in range(2):
                act.wait_ge(s_out[k], 16 * NU + 16 + 16)

        @block.tensor
        def _(pe):
            pe.wait_ge(const_in, 48)
            with pe.Fori(0, NU // 2) as i:
                for k in range(2):
                    un = 2 * i + k
                    pe.wait_ge(x1_ready, un + 1)
                    for n in range(4):
                        pe.wait_ge(x1c_ready, 4 * un + n + 1)
                        for m4 in range(4):
                            m = pe.transpose(pt[:, n, m4 * P:m4 * P + P],
                                             xt[:, k, 2 * n + m4 // 2, m4 % 2, :], ident[:])
                        m.then_inc(turned, 1)
                    pe.wait_ge(u_ready, un + 3)
                    for n in range(4):
                        for half, free in ((0, so_a), (1, so_ready)):
                            pe.wait_ge(free, 4 * un + n + 1)
                            pe.matmul(pf[:, 2 * (n % 2) + half, :], d1[:, half * P:half * P + P],
                                      u[:, k, 2 * n:2 * n + 2].rearrange("p h q c -> p (h q c)"),
                                      start=True, stop=True).then_inc(f_done, 1)
            for n in range(2):
                for half, free in ((0, so_a), (1, so_ready)):
                    pe.wait_ge(free, 4 * NU + n + 1)
                    pe.matmul(pf[:, 2 * n + half, 0:16 * KX], d1[:, half * P:half * P + P],
                              ph[:, 8 * n:8 * n + 8, :].rearrange("p h m -> p (h m)"),
                              start=True, stop=True).then_inc(f_done, 1)


def filters(nc, I, S):
    with Arena(nc, "flt") as A:
        sp_ = A.sb("sp", [P, 2, 2, 2 * KX])
        fw = A.sb("fw", [P, 2, 2, 2, NF2])
        vv = A.sb("vv", [KX, 2, 2 * NF2])
        tmp = A.sb("tmp", [KX, 2, 2 * NF2])
        parts = A.sb("parts", [KX, 2, 3, 2, 2 * NF2], BF16)
        pv = A.ps("pv", [KX, 2, 2, 256])
        loads = [A.sem(f"loads{k}") for k in range(2)]
        outs = [A.sem(f"outs{k}") for k in range(2)]
        v_done, chain, parts_ready = A.sem("v_done"), A.sem("chain"), A.sem("parts_ready")
        block = A.ctx.enter_context(nc.Block())
        spx = S["SP"]

        @block.sync
        def _(sp):
            for f in range(NF1):
                k = f % 2
                if f >= 2:
                    sp.wait_ge(v_done, f - 1)
                sp.dma_start(sp_[:, k, 0], spx[f]).then_inc(loads[k], 16)
                sp.dma_start(sp_[:, k, 1], spx[16 + f]).then_inc(loads[k], 16)
                sp.dma_start(fw[:, k], I["fw"][f].rearrange("b (p s f) -> b p s f", p=2, s=4)[:, :, 0:2]).then_inc(loads[k], 16)

        @block.tensor
        def _(pe):
            for f in range(NF1):
                k = f % 2
                pe.wait_ge(loads[k], 48 * (f // 2) + 48)
                if f >= 2:
                    pe.wait_ge(chain, 4 * (f - 1))
                for x in range(2):
                    for part in range(2):
                        m = pe.matmul(pv[:, k, x], sp_[:, k, part, x * KX:x * KX + KX],
                                      fw[:, k, part].rearrange("b s f -> b (s f)"), start=part == 0, stop=part == 1)
                m.then_inc(v_done, 1)

        @block.vector
        def _(v):
            n = [0]

            def step(ins):
                n[0] += 1
                ins.then_inc(chain, 1)
                v.wait_ge(chain, n[0])

            for f in range(NF1):
                k = f % 2
                v.wait_ge(v_done, f + 1)
                if f >= 2:
                    v.wait_ge(outs[k], 48 * (f // 2))
                split3(v, pv[:, k], tmp[:], parts[:, k, 0], parts[:, k, 1], parts[:, k, 2], step)
                v.sem_inc(parts_ready, 1)

        @block.scalar
        def _(act):
            for f in range(NF1):
                k = f % 2
                act.wait_ge(parts_ready, f + 1)
                for s in range(3):
                    act.dma_start(S["VS"][s, f].rearrange("k x c f -> k x (c f)"), parts[:, k, s]).then_inc(outs[k], 16)
            for k in range(2):
                act.wait_ge(outs[k], 48 * ((NF1 + 1 - k) // 2))


V_PARTS, A_PARTS = (0, 0, 1, 0, 1, 2), (0, 1, 0, 2, 1, 0)
KROWS = KX * len(V_PARTS)


def spectrum(nc, I, S):
    NTL = NF2 // FT
    UF = 12 * NB
    with Arena(nc, "spc") as A:
        AS = A.sb("as", [KROWS, 2, C, C], BF16)
        V = A.sb("v", [KROWS, 2, 2, 2, NF2], BF16)
        G = A.sb("g", [P, FT, 4, C])
        U = A.sb("u", [P, 2, NF2 * UF + 32])
        Ss = A.sb("s", [P, 2, 2, NB, 2 * C])
        F = A.sb("f", [P, 2, 2, 4, NF2])
        yo = A.sb("yo", [P, 8, C])
        pg = A.ps("pg", [P, 4, 512])
        pu = A.ps("pu", [P, 2, 512])
        py = A.ps("py", [P, 2, 4, C])
        as_in = A.sem("as_in")
        in_v = [A.sem(f"in_v{k}") for k in range(2)]
        in_s = [A.sem(f"in_s{k}") for k in range(2)]
        u_done, u_ready = A.sem("u_done"), A.sem("u_ready")
        g_done, ga, gd = A.sem("g_done"), A.sem("ga"), A.sem("gd")
        y_done, ya, yd = A.sem("y_done"), A.sem("ya"), A.sem("yd")
        y_out, pad_ready = A.sem("y_out"), A.sem("pad_ready")
        block = A.ctx.enter_context(nc.Block())

        def one(ap, i):
            if isinstance(i, int):
                return ap[i]
            n = len(ap.shape)
            names = [f"x{k}" for k in range(n)]
            return ap[bass.ds(i, 1)].rearrange(f"{' '.join(names)} -> ({names[0]} {names[1]}) {' '.join(names[2:])}")

        @block.gpsimd
        def _(sp):
            for g, part in enumerate(A_PARTS):
                for x in range(2):
                    sp.dma_start(AS[KX * g:KX * g + KX, x].rearrange("k e d -> k (e d)"),
                                 S["AS"][x, part].rearrange("k d e -> k (d e)")).then_inc(as_in, 16)

            def load(f, k):
                for g, part in enumerate(V_PARTS):
                    sp.dma_start(V[KX * g:KX * g + KX, k].rearrange("k x c f -> k (x c f)"),
                                 one(S["VS"][part], f).rearrange("k x c f -> k (x c f)")).then_inc(in_v[k], 16)
                sp.dma_start(F[:, k].rearrange("b p s f -> b (p s f)"), one(I["fw"], f)).then_inc(in_s[k], 16)
                for part in range(2):
                    src = S["SF"].rearrange("n f b m -> f b n m")
                    sp.dma_start(Ss[:, k, part], one(src, f + 16 * part)).then_inc(in_s[k], 16)

            load(0, 0)
            load(1, 1)
            with sp.Fori(0, NF1 // 2) as i:
                for k in range(2):
                    f = 2 * i + k
                    sp.wait_ge(u_done, 3 * NB * (f + 1))
                    sp.wait_ge(g_done, 32 * NTL * (f + 1))
                    load((f + 2) % NF1, k)
            for k in range(2):
                sp.wait_ge(in_v[k], 96 * (NF1 // 2 + 1))
                sp.wait_ge(in_s[k], 48 * (NF1 // 2 + 1))

        @block.tensor
        def _(pe):
            def second_step(f, k, unit):
                b, g = divmod(unit, 3)
                ph = 0 if g == 1 else 1
                fo = 2 if g == 0 else 0
                n = 3 * NB * f + unit
                pe.wait_ge(u_ready, n + 1)
                for part in range(2):
                    m = pe.matmul(pu[:, unit % 2, 0:2 * NF2], Ss[:, k, part, b, ph * C:ph * C + C],
                                  F[:, k, part, fo:fo + 2].rearrange("b s f -> b (s f)"),
                                  start=part == 0, stop=part == 1)
                m.then_inc(u_done, 1)

            def make_g(f, k, t):
                n = NTL * f + t
                for j in range(32):
                    pe.wait_ge(ga if j % 2 == 0 else gd, 16 * n + j // 2 + 1)
                    for e in range(4):
                        for x in range(2):
                            m = pe.matmul(pg[:, j % 4, 128 * e + 64 * x:128 * e + 64 * x + 64],
                                          AS[:, x, :, 4 * j + e],
                                          V[:, k, x, :, FT * t:FT * t + FT], start=True, stop=True)
                    m.then_inc(g_done, 1)

            def make_y(f, k, t):
                n = NTL * f + t
                if t == 0:
                    pe.wait_ge(u_ready, 3 * NB * (f + 1) + 2)
                pe.wait_ge(ga, 16 * n + 18)
                pe.wait_ge(gd, 16 * n + 18)
                for g in range(8):
                    if g % 4 == 0:
                        pe.wait_ge(ya if g == 0 else yd, n + 1)
                    for c, base in enumerate((8, 2, 6, 0)):
                        for j in range(4):
                            fr = FT * t + 4 * g + j
                            w = U[:, k, UF * fr + NB * base:UF * fr + NB * base + 32]
                            m = pe.matmul(py[32 * j:32 * j + 32, g // 4, g % 4, :], w, G[:, 4 * g + j, c, :],
                                          start=c == 0, stop=c == 3, skip_group_check=True)
                    if g % 4 == 3:
                        m.then_inc(y_done, 1)

            pe.wait_ge(in_s[0], 48)
            for unit in range(3 * NB):
                second_step(0, 0, unit)
            pe.wait_ge(as_in, 16 * 12)
            pe.wait_ge(pad_ready, 1)

            def body(f, k, i, last):
                pe.wait_ge(in_v[k], 96 * (f // 2) + 96 if isinstance(f, int) else 96 * i + 96)
                for t in range(NTL):
                    if not last:
                        if t == 0:
                            pe.wait_ge(in_s[1 - k], 48 * i + 48 + 48 * k)
                        for unit in range(3 * t, 3 * t + 3):
                            second_step(f + 1, 1 - k, unit)
                    make_g(f, k, t)
                    make_y(f, k, t)

            with pe.Fori(0, NF1 // 2) as i:
                for k in range(2):
                    body(2 * i + k, k, i, False)
            body(NF1 - 1, 0, NF1 // 2, True)

        def g_out(j):
            return G[:, :, :, 4 * j:4 * j + 4].rearrange("d f c e -> d e c f")

        def g_in(j):
            return pg[:, j % 4, :].rearrange("d (e c f) -> d e c f", e=4, c=4)

        def f_loop(eng, body):
            with eng.Fori(0, NF1 // 2) as i:
                for k in range(2):
                    body(2 * i + k, k, False)
            body(NF1 - 1, 0, True)

        @block.scalar
        def _(act):
            act.sem_inc(u_ready, 2)
            act.sem_inc(ga, 2)
            act.sem_inc(gd, 2)
            act.sem_inc(ya, 1)
            act.sem_inc(yd, 1)
            act.sem_inc(y_done, 1)
            act.sem_inc(y_out, 64)

            def u_out(f, k, unit):
                b, g = divmod(unit, 3)
                act.wait_ge(u_done, 3 * NB * f + unit + 1)
                dst = U[:, k, 0:NF2 * UF].rearrange("d (f s b) -> d b s f", s=12, b=NB)[:, b]
                src = pu[:, unit % 2, 0:2 * NF2]
                act.activation(dst[:, 2 * g], src[:, NF2:], ACT.Copy, scale=-1.0)
                act.activation(dst[:, 2 * g + 1], src[:, 0:NF2], ACT.Copy)
                act.activation(dst[:, 2 * g + 6:2 * g + 8], src.rearrange("d (s f) -> d s f", s=2),
                               ACT.Copy).then_inc(u_ready, 1)

            for unit in range(3 * NB):
                u_out(0, 0, unit)

            def body(f, k, last):
                for t in range(NTL):
                    n = NTL * f + t
                    if not last:
                        act.wait_ge(y_done, 2 * NTL * f + 1)
                        for unit in range(3 * t, 3 * t + 3):
                            u_out(f + 1, 1 - k, unit)
                    act.wait_ge(y_done, 2 * n + 1)
                    for j in range(0, 32, 2):
                        act.wait_ge(g_done, 32 * n + j + 1)
                        act.activation(g_out(j), g_in(j), ACT.Copy).then_inc(ga, 1)
                    act.wait_ge(y_out, 64 * n + 64)
                    act.wait_ge(y_done, 2 * n + 2)
                    act.activation(yo[:, 0:4, :], py[:, 0], ACT.Copy).then_inc(ya, 1)

            f_loop(act, body)

        @block.vector
        def _(v):
            v.memset(U[:, :, NF2 * UF:], 0.0).then_inc(pad_ready, 1)

            def body(f, k, last):
                for t in range(NTL):
                    n = NTL * f + t
                    v.wait_ge(y_done, 2 * n + 1)
                    for j in range(1, 32, 2):
                        v.wait_ge(g_done, 32 * n + j + 1)
                        v.tensor_copy(g_out(j), g_in(j)).then_inc(gd, 1)
                    v.wait_ge(y_out, 64 * n + 64)
                    v.wait_ge(y_done, 2 * n + 3)
                    v.tensor_copy(yo[:, 4:8, :], py[:, 1]).then_inc(yd, 1)

            f_loop(v, body)

        @block.sync
        def _(sp):
            dst = S["YD"].rearrange("f (t g j) r e -> f t j r g e", t=NTL, j=4)

            def body(f, k, last):
                for t in range(NTL):
                    n = NTL * f + t
                    sp.wait_ge(ya, n + 2)
                    sp.wait_ge(yd, n + 2)
                    for j in range(4):
                        sp.dma_start(one(dst[:, t, j], f), yo[32 * j:32 * j + 16]).then_inc(y_out, 16)

            f_loop(sp, body)
            sp.wait_ge(y_out, 64 * NF1 * NTL + 64)


def inverse(nc, I, S):
    with Arena(nc, "ivs") as A:
        Y = A.sb("y", [P, 2, 2, 2, CH])
        F = A.sb("f", [P, 2, 3, P])
        to = A.sb("to", [P, 2, 2, 2 * CH])
        pt = A.ps("pt", [P, 2, 2, 2 * CH])
        loads = [A.sem(f"loads{k}") for k in range(2)]
        t_out = [A.sem(f"t_out{k}") for k in range(2)]
        t_done, tr, ti = A.sem("t_done"), A.sem("tr"), A.sem("ti")
        block = A.ctx.enter_context(nc.Block())

        def f_loop(eng, body):
            with eng.Fori(0, NF1 // 2) as i:
                for k in range(2):
                    body(2 * i + k, k, i)
            body(NF1 - 1, 0, NF1 // 2)

        def at(ap, f):
            return ap[f] if isinstance(f, int) else ap[bass.ds(f, 1)].rearrange("o p m -> (o p) m")

        @block.gpsimd
        def _(pool):
            def body(f, k, i):
                pool.wait_ge(t_done, 2 * f + 2)
                pool.dma_start(Y[:, k].rearrange("p x c m -> p (x c m)"),
                               at(S["YD"].rearrange("f p r e -> f p (r e)"), f)).then_inc(loads[k], 16)
                pool.dma_start(F[:, k].rearrange("p s b -> p (s b)"), at(I["fi"], f)).then_inc(loads[k], 16)

            f_loop(pool, body)

        @block.tensor
        def _(pe):
            pe.sem_inc(t_done, 4)

            def body(f, k, i):
                pe.wait_ge(loads[k], 32 * i + 32)
                for c, free in ((0, tr), (1, ti)):
                    pe.wait_ge(free, f + 1)
                    for x in range(2):
                        for part, w in enumerate(((0, 2), (1, 0))[c]):
                            m = pe.matmul(pt[:, k, c, CH * x:CH * x + CH], F[:, k, w, :], Y[:, k, x, part, :],
                                          start=part == 0, stop=part == 1)
                    m.then_inc(t_done, 1)

            f_loop(pe, body)

        @block.scalar
        def _(act):
            act.sem_inc(tr, 2)
            act.sem_inc(ti, 2)
            act.sem_inc(t_out[0], 32)
            act.sem_inc(t_out[1], 32)

            def body(f, k, i):
                act.wait_ge(t_out[k], 32 * i + 32)
                act.wait_ge(t_done, 2 * f + 5)
                act.activation(to[:, k, 0, :], pt[:, k, 0, :], ACT.Copy).then_inc(tr, 1)

            f_loop(act, body)

        @block.vector
        def _(v):
            def body(f, k, i):
                v.wait_ge(t_out[k], 32 * i + 32)
                v.wait_ge(t_done, 2 * f + 6)
                v.tensor_copy(to[:, k, 1, :], pt[:, k, 1, :]).then_inc(ti, 1)

            f_loop(v, body)

        @block.sync
        def _(sp):
            def body(f, k, i):
                for c, ready in ((0, tr), (1, ti)):
                    sp.wait_ge(ready, f + 3)
                    sp.dma_start(at(S["TD"], f + 16 * c), to[:, k, c, :]).then_inc(t_out[k], 16)

            f_loop(sp, body)
            for k in range(2):
                sp.wait_ge(t_out[k], 32 * (NF1 // 2 + 1 - k) + 32)


def tokens_back(nc, I, S, X):
    HB = 32
    with Arena(nc, "bck") as A:
        d2 = A.sb("d2", [P, 64])
        Tt = A.sb("t", [P, 2, 2 * NB * C])
        px = A.ps("px", [P, 2, 8, 64])
        const_in = A.sem("const_in")
        loads = [A.sem(f"loads{k}") for k in range(2)]
        x_done, x_added = A.sem("x_done"), A.sem("x_added")
        block = A.ctx.enter_context(nc.Block())

        @block.sync
        def _(sp):
            sp.dma_start(d2[:], S["D2M"]).then_inc(const_in, 16)
            sp.dma_start(X[:].rearrange("c (b t) -> c b t", b=NB),
                         S["X1C"].rearrange("b c t -> c b t")).then_inc(const_in, 16)

        @block.gpsimd
        def _(pool):
            src = S["TD"][0:32].rearrange("f (l h) m -> h (f l) m", l=4)
            with pool.Fori(0, HB // 2) as i:
                for k in range(2):
                    pool.wait_ge(x_done, 2 * i + k + 1)
                    pool.dma_start(Tt[:, k], src[bass.ds(2 * i + k, 1)].rearrange("o q m -> (o q) m")).then_inc(loads[k], 16)

        @block.tensor
        def _(pe):
            pe.sem_inc(x_done, 2)
            pe.wait_ge(const_in, 32)
            with pe.Fori(0, HB // 2) as i:
                for k in range(2):
                    pe.wait_ge(loads[k], 16 * i + 16)
                    pe.wait_ge(x_added, 2 * i + k + 1)
                    for n in range(8):
                        m = pe.matmul(px[:, k, n, :], Tt[:, k, C * n:C * n + C], d2[:], start=True, stop=True)
                    m.then_inc(x_done, 1)

        @block.vector
        def _(v):
            v.sem_inc(x_added, 2)
            v.wait_ge(const_in, 32)
            with v.Fori(0, HB // 2) as i:
                for k in range(2):
                    v.wait_ge(x_done, 2 * i + k + 3)
                    xs = X[:].rearrange("c (b q h x) -> c h x b q", b=NB, q=64, x=2)[:, bass.ds(2 * i + k, 1)].rearrange(
                        "c o x b q -> c (o x) b q")
                    v.tensor_tensor(xs, px[:, k].rearrange("c (x b) q -> c x b q", x=2), xs, ALU.add).then_inc(x_added, 1)


def ln_tensor(pe, onesm, src, pm, pvar, sq, s, n, credit=0):
    for j in range(2):
        pe.wait_ge(s["src"], 2 * n + j + 1 + credit)
        pe.wait_ge(s["d"], 2 * n + j + 1)
        pe.matmul(pm[:, j], onesm[:], src(j), start=True, stop=True).then_inc(s["mean"], 1)
    for j in range(2):
        pe.wait_ge(s["sq"], 2 * n + j + 1)
        pe.wait_ge(s["sd"], 2 * n + j + 1)
        pe.matmul(pvar[:, j], onesm[:], sq[:, j], start=True, stop=True).then_inc(s["var"], 1)


def ln_vector(v, src, pm, d, sd, out, s, n):
    for j in range(2):
        v.wait_ge(s["mean"], 2 * n + j + 1)
        v.wait_ge(s["out"], 2 * n + j + 1)
        v.tensor_tensor(d[:, j], src(j), pm[:, j], ALU.subtract).then_inc(s["d"], 1)
    for j in range(2):
        v.wait_ge(s["sd"], 2 * n + j + 3)
        v.reciprocal(sd[:, j], sd[:, j]).then_inc(s["rs"], 1)
    for j in range(2):
        v.wait_ge(s["rs"], 2 * n + j + 1)
        v.tensor_tensor(out(j), d[:, j], sd[:, j], ALU.mult).then_inc(s["out"], 1)


def ln_scalar(act, d, sq, sd, pvar, eps, s, n):
    for j in range(2):
        act.wait_ge(s["d"], 2 * n + j + 3)
        act.wait_ge(s["var"], 2 * n + j + 1)
        act.activation(sq[:, j], d[:, j], ACT.Square).then_inc(s["sq"], 1)
    for j in range(2):
        act.wait_ge(s["var"], 2 * n + j + 3)
        act.wait_ge(s["out"], 2 * n + j + 1)
        act.activation(sd[:, j], pvar[:, j], ACT.Sqrt, bias=eps[:]).then_inc(s["sd"], 1)


def ln_sems(A, tag):
    return {k: A.sem(f"{tag}_{k}") for k in ("src", "mean", "d", "sq", "var", "sd", "rs", "out")}


def second_norm(nc, I, X, XN, pool4):
    NQ = NB * NCH
    with Arena(nc, "ln2") as A:
        onesm = A.sb("onesm", [P, P])
        eps = A.sb("eps", [P, 1])
        d = A.sb("d", [P, 2, CH])
        sq = A.sb("sq", [P, 2, CH])
        sd = A.sb("sd", [P, 2, CH])
        pm = A.ps("pm", [P, 2, CH])
        pvar = A.ps("pvar", [P, 2, CH])
        s = ln_sems(A, "s")
        set_up, pooled = A.sem("set_up"), A.sem("pooled")
        block = A.ctx.enter_context(nc.Block())

        def chunk(T_, i, j):
            return T_[:, bass.ds((2 * i + j) * CH, CH)]

        @block.gpsimd
        def _(pool):
            pool.memset(onesm[:], 1.0 / C).then_inc(set_up, 1)
            pool.memset(eps[:], EPS_C).then_inc(set_up, 1)
            pool.sem_inc(s["src"], NQ)
            for name in ("d", "var", "sd", "out"):
                pool.sem_inc(s[name], 2)

        @block.tensor
        def _(pe):
            pe.wait_ge(set_up, 2)
            with pe.Fori(0, NQ // 2) as i:
                ln_tensor(pe, onesm, lambda j: chunk(X, i, j), pm, pvar, sq, s, i)

        @block.scalar
        def _(act):
            act.wait_ge(set_up, 2)
            with act.Fori(0, NQ // 2) as i:
                ln_scalar(act, d, sq, sd, pvar, eps, s, i)

        @block.vector
        def _(v):
            with v.Fori(0, NQ // 2) as i:
                ln_vector(v, lambda j: chunk(X, i, j), pm, d, sd, lambda j: chunk(XN, i, j), s, i)
                for j in range(2):
                    v.wait_ge(s["out"], 2 * i + j + 3)
                    v.tensor_reduce(pool4[:, bass.ds((2 * i + j) * 32, 32)],
                                    chunk(XN, i, j).rearrange("c (r w) -> c r w", w=16), AX.X, ALU.add)


def gates(nc, I, XN, pool4, cosp, ci):
    with Arena(nc, "gat") as A:
        wsp, bsp = A.sb("wsp", [16, 9]), A.sb("bsp", [9, 1])
        wo1, bo1, wo2, bo2 = A.sb("wo1", [P, 8]), A.sb("bo1", [8, 1]), A.sb("wo2", [8, C]), A.sb("bo2", [9, C])
        wi1, bi1, wi2, bi2 = A.sb("wi1", [P, 8]), A.sb("bi1", [8, 1]), A.sb("wi2", [8, C]), A.sb("bi2", [P, 1])
        onek = A.sb("onek", [P, 1])
        p16 = A.sb("p16", [P, NB, 16])
        gap = A.sb("gap", [P, NB])
        gaps = A.sb("gaps", [P, NB])
        xs, sp_ = A.sb("xs", [16, NB]), A.sb("sp", [9, NB])
        ho, hi, hob = A.sb("ho", [8, NB]), A.sb("hi", [8, NB]), A.sb("hob", [8, NB, 9])
        ct = A.sb("ct", [9, NB, C])
        ps = A.ps("ps", [P, 512])
        pq = A.ps("pq", [P, 512])
        pr = A.ps("pr", [P, 512])
        w_in, chain, pe_done = A.sem("w_in"), A.sem("chain"), A.sem("pe_done")
        block = A.ctx.enter_context(nc.Block())

        @block.sync
        def _(sp):
            for dst, name in ((wsp, "W_sp"), (bsp, "b_sp"), (wo1, "W_o1"), (bo1, "b_o1"), (wo2, "W_o2"),
                              (wi1, "W_i1"), (bi1, "b_i1"), (wi2, "W_i2"), (bi2, "b_i2")):
                sp.dma_start(dst[:], I[name]).then_inc(w_in, 16)
            sp.dma_start(bo2[:], I["b_o2"].partition_broadcast(9)).then_inc(w_in, 16)
            sp.wait_ge(w_in, 160)

        @block.vector
        def _(v):
            n = [0]

            def step(ins):
                n[0] += 1
                ins.then_inc(chain, 1)
                v.wait_ge(chain, n[0])

            v.wait_ge(w_in, 160)
            step(v.memset(onek[:], 1.0 / (C * 256)))
            step(v.tensor_reduce(p16[:].rearrange("c b (y x) -> c (b y) x", x=4),
                                 pool4[:].rearrange("c (q r x) -> c q x r", r=16, x=4), AX.X, ALU.add))
            step(v.tensor_reduce(gaps[:], p16[:], AX.X, ALU.add))
            step(v.tensor_scalar(gap[:], gaps[:], 1.0 / T, None, ALU.mult))
            v.wait_ge(pe_done, 1)
            step(v.tensor_copy(xs[:], ps[0:16, 0:NB]))
            step(v.tensor_scalar(ho[:], ps[0:8, 8:8 + NB], bo1[:], 0.0, ALU.add, ALU.max))
            step(v.tensor_scalar(hi[:], ps[0:8, 16:16 + NB], bi1[:], 0.0, ALU.add, ALU.max))
            step(v.tensor_copy(hob[:], ho[:].rearrange("p (b o) -> p b o", o=1).to_broadcast([8, NB, 9])))
            v.wait_ge(pe_done, 2)
            step(v.tensor_scalar(sp_[:], pq[0:9, 0:NB], bsp[:], None, ALU.add))
            step(v.tensor_scalar(ci[:], pq[:, 8:8 + NB], bi2[:], None, ALU.add))
            for b in range(NB):
                step(v.tensor_tensor(ct[:, b], pr[0:9, C * b:C * b + C], bo2[:], ALU.add))
                step(v.tensor_scalar(cosp[:, b], ct[:, b], sp_[:, b:b + 1], None, ALU.mult))

        @block.tensor
        def _(pe):
            pe.wait_ge(chain, 4)
            pe.wait_ge(w_in, 160)
            for b in range(NB):
                pe.matmul(ps[0:16, b:b + 1], p16[:, b], onek[:], start=True, stop=True)
            pe.matmul(ps[0:8, 8:8 + NB], wo1[:], gap[:], start=True, stop=True)
            pe.matmul(ps[0:8, 16:16 + NB], wi1[:], gap[:], start=True, stop=True).then_inc(pe_done, 1)
            pe.wait_ge(chain, 8)
            pe.matmul(pq[0:9, 0:NB], wsp[:], xs[:], start=True, stop=True)
            pe.matmul(pq[:, 8:8 + NB], wi2[:], hi[:], start=True, stop=True)
            for b in range(NB):
                m = pe.matmul(pr[0:9, C * b:C * b + C], hob[:, b], wo2[:], start=True, stop=True)
            m.then_inc(pe_done, 1)


def image(nc, S, XN, ci):
    with Arena(nc, "img") as A:
        vr = A.sb("vr", [1, 4, CH])
        pv = A.ps("pv", [1, 4, CH])
        v_done, vr_ready = A.sem("v_done"), A.sem("vr_ready")
        v_out = [A.sem(f"v_out{k}") for k in range(4)]
        block = A.ctx.enter_context(nc.Block())

        @block.tensor
        def _(pe):
            for q in range(NB * NCH):
                if q >= 4:
                    pe.wait_ge(vr_ready, q - 3)
                pe.matmul(pv[:, q % 4], ci[:, q // NCH:q // NCH + 1], XN[:, CH * q:CH * q + CH],
                          start=True, stop=True).then_inc(v_done, 1)

        @block.scalar
        def _(act):
            for q in range(NB * NCH):
                act.wait_ge(v_done, q + 1)
                if q >= 4:
                    act.wait_ge(v_out[q % 4], 16 * (q // 4))
                act.activation(vr[:, q % 4], pv[:, q % 4], ACT.Copy).then_inc(vr_ready, 1)

        @block.sync
        def _(sp):
            for q in range(NB * NCH):
                b, n = divmod(q, NCH)
                sp.wait_ge(vr_ready, q + 1)
                sp.dma_start(S["VP"][8 * n + 1:8 * n + 9, b, 1:65], 
                             vr[:, q % 4].rearrange("o (h w) -> o h w", w=W)).then_inc(v_out[q % 4], 16)
            for k in range(4):
                sp.wait_ge(v_out[k], 16 * (NB * NCH // 4))


def experts(nc, I, S, X, cosp, out):
    GR = 2048
    NGR, GC, GT = NB * T // GR, GR // CH, GR // P
    NCHAIN = 20
    with Arena(nc, "moe") as A:
        ident, onesm, eps = A.sb("ident", [P, P]), A.sb("onesm", [P, P]), A.sb("eps", [P, 1])
        ew, rw = A.sb("ew", [P, NE * C]), A.sb("rw", [P, NE])
        rb, prio = A.sb("rb", [P, NE]), A.sb("prio", [P, NE])
        eb = A.sb("eb", [P, GT, C])
        v9, cs = A.sb("v9", [9, 32, W]), A.sb("cs", [9, C])
        x3 = A.sb("x3", [P, GC, CH])
        z = A.sb("z", [P, GC, CH])
        d, sq, sd = A.sb("d", [P, 2, CH]), A.sb("sq", [P, 2, CH]), A.sb("sd", [P, 2, CH])
        gb = A.sb("gb", [P, 8, GT, NE])
        g1 = A.sb("g1", [P, 8, GT])
        gt = A.sb("gt", [P, P])
        yt = A.sb("yt", [P, 2, 2, C])
        fin = A.sb("fin", [P, 2, CH])
        ex = A.ps("ex", [P, 4, CH])
        pl = A.ps("pl", [P, CH])
        pf = A.ps("pf", [P, CH])
        pm, pvar = ex[:, 0:2], ex[:, 2:4]
        const_in, set_up, v9_in = A.sem("const_in"), A.sem("set_up"), A.sem("v9_in")
        s = ln_sems(A, "s")
        cs_ready, conv_done, lg_done = A.sem("cs_ready"), A.sem("conv_done"), A.sem("lg_done")
        arg_ready, exp_ready, gate_ready = A.sem("arg_ready"), A.sem("exp_ready"), A.sem("gate_ready")
        gt_turned, gt_ready, chain = A.sem("gt_turned"), A.sem("gt_ready"), A.sem("chain")
        mixed, yt_used, fin_ready = A.sem("mixed"), A.sem("yt_used"), A.sem("fin_ready")
        outs = [A.sem(f"outs{k}") for k in range(2)]
        block = A.ctx.enter_context(nc.Block())

        @block.sync
        def _(sp):
            for dst, src in ((ident[:], I["ident"]), (ew[:], I["expert_w"]), (rw[:], I["router_w"]),
                             (rb[:], I["router_b"].partition_broadcast(P)), (prio[:], I["prio8"])):
                sp.dma_start(dst, src).then_inc(const_in, 16)
            sp.wait_ge(set_up, 3)
            for t in range(GT):
                sp.dma_start(eb[NE * t:NE * t + NE, t, :], I["expert_b"]).then_inc(const_in, 16)
            dst = out.rearrange("b c (h n m) -> b h n c m", h=2, n=GC)
            with sp.Fori(0, NGR) as i:
                for n in range(GC):
                    sp.wait_ge(fin_ready, GC * i + n + 3)
                    sp.dma_start(dst[bass.ds(i // 2, 1), bass.ds(i % 2, 1), n].rearrange(
                        "o a c m -> (o a c) m"), fin[:, n % 2]).then_inc(outs[n % 2], 16)
            for k in range(2):
                sp.wait_ge(outs[k], 16 * NGR * GC // 2 + 16)

        @block.gpsimd
        def _(pool):
            pool.memset(eb[:], 0.0).then_inc(set_up, 1)
            pool.memset(onesm[:], 1.0 / C).then_inc(set_up, 1)
            pool.memset(eps[:], EPS_T).then_inc(set_up, 1)
            for name in ("d", "var", "sd", "out"):
                pool.sem_inc(s[name], 2)
            pool.sem_inc(s["src"], 1)
            pool.sem_inc(conv_done, GC)
            pool.sem_inc(fin_ready, 2)
            pool.sem_inc(yt_used, 2)
            pool.sem_inc(mixed, 2 * NE)
            rows = S["VP"].rearrange("h b w -> b h w")
            with pool.Fori(0, NGR) as i:
                pool.wait_ge(conv_done, GC * i + GC)
                for ti in range(3):
                    src = rows[bass.ds(i // 2, 1), bass.ds((i % 2) * 32 + ti, 32), :]
                    for tj in range(3):
                        pool.dma_start(v9[3 * ti + tj:3 * ti + tj + 1], src[:, :, tj:tj + W]).then_inc(v9_in, 16)

        @block.tensor
        def _(pe):
            def final(i, t):
                if t == 0:
                    pe.wait_ge(gt_ready, i + 1)
                if t % 4 == 0:
                    pe.wait_ge(fin_ready, GC * i + t // 4 + 2)
                pe.wait_ge(mixed, NE * (GT * i + t) + 3 * NE)
                o = pf[:, P * (t % 4):P * (t % 4) + P]
                pe.matmul(o, yt[:, t % 2, 0], ident[:], start=True, stop=False)
                pe.matmul(o, yt[:, t % 2, 1], ident[:], start=False, stop=False)
                pe.matmul(o, eb[:, t], gt[:], start=False, stop=True).then_inc(yt_used, 1)

            pe.wait_ge(const_in, 16 * (5 + GT))
            pe.wait_ge(set_up, 3)
            with pe.Fori(0, NGR) as i:
                pe.wait_ge(v9_in, 144 * i + 144)
                pe.wait_ge(cs_ready, i + 1)
                pe.wait_ge(fin_ready, GC * i + 2)
                pe.wait_ge(mixed, NE * GT * i + 2 * NE)
                for h in range(GC // 2):
                    for j in range(2):
                        n = 2 * h + j
                        pe.wait_ge(s["src"], GC * i + n + 1)
                        pe.matmul(pf[:], cs[:], v9[:, 8 * n:8 * n + 8, :].rearrange("p h w -> p (h w)"),
                                  start=True, stop=True).then_inc(conv_done, 1)
                    ln_tensor(pe, onesm, lambda j: x3[:, 2 * h + j], pm, pvar, sq, s, (GC // 2) * i + h, 1)
                pe.wait_ge(s["out"], GC * i + GC + 2)
                for t in range(GT):
                    m = pe.matmul(pl[:, NE * t:NE * t + NE], z[:, t // 4, P * (t % 4):P * (t % 4) + P], rw[:],
                                  start=True, stop=True)
                m.then_inc(lg_done, 1)
                for t in range(GT):
                    pe.wait_ge(mixed, NE * (GT * i + t) + NE)
                    for k in range(2):
                        m = pe.matmul(ex[:, 2 * (t % 2) + k], z[:, t // 4, P * (t % 4):P * (t % 4) + P],
                                      ew[:, CH * k:CH * k + CH], start=True, stop=True)
                    m.then_inc(lg_done, 1)
                    if t == 1:
                        pe.wait_ge(gate_ready, i + 1)
                        pe.transpose(pl[:, P:2 * P], gb[:, 7].rearrange("p t e -> p (t e)"), ident[:]).then_inc(gt_turned, 1)
                    if t:
                        final(i, t - 1)
                final(i, GT - 1)

        @block.scalar
        def _(act):
            act.sem_inc(outs[0], 16)
            act.sem_inc(outs[1], 16)
            act.wait_ge(set_up, 3)
            with act.Fori(0, NGR) as i:
                act.wait_ge(conv_done, GC * i + GC)
                act.activation(cs[:], cosp[:, bass.ds(i // 2, 1), :].rearrange("p o c -> p (o c)"), ACT.Copy).then_inc(cs_ready, 1)
                for h in range(GC // 2):
                    ln_scalar(act, d, sq, sd, pvar, eps, s, (GC // 2) * i + h)
                act.wait_ge(arg_ready, i + 1)
                act.activation(gb[:, 2], gb[:, 1], ACT.Exp).then_inc(exp_ready, 1)
                act.wait_ge(gt_turned, i + 1)
                act.activation(gt[:], pl[:, P:2 * P], ACT.Copy).then_inc(gt_ready, 1)

        @block.vector
        def _(v):
            def bc(col):
                return g1[:, col].rearrange("p (t o) -> p t o", o=1).to_broadcast([P, GT, NE])

            def row(a):
                return a[:].rearrange("p (o e) -> p o e", o=1).to_broadcast([P, GT, NE])

            def gate(i):
                n = [0]

                def step(ins):
                    n[0] += 1
                    ins.then_inc(chain, 1)
                    v.wait_ge(chain, NCHAIN * i + n[0])

                v.wait_ge(lg_done, (GT + 1) * i + 1)
                step(v.tensor_tensor(gb[:, 0], pl[:, 0:GT * NE].rearrange("p (t e) -> p t e", e=NE), row(rb), ALU.add))
                step(v.tensor_reduce(g1[:, 0], gb[:, 0], AX.X, ALU.max))
                v.tensor_tensor(gb[:, 1], gb[:, 0], bc(0), ALU.subtract).then_inc(arg_ready, 1)
                v.wait_ge(exp_ready, i + 1)
                step(v.tensor_reduce(g1[:, 1], gb[:, 2], AX.X, ALU.add))
                step(v.reciprocal(g1[:, 2], g1[:, 1]))
                step(v.tensor_tensor(gb[:, 3], gb[:, 2], bc(2), ALU.mult))
                for r, (src, col, hot) in enumerate(((3, 3, 6), (4, 5, 5))):
                    step(v.tensor_reduce(g1[:, col], gb[:, src], AX.X, ALU.max))
                    step(v.tensor_tensor(gb[:, 5], gb[:, src], bc(col), ALU.is_equal))
                    step(v.tensor_tensor(gb[:, 5], gb[:, 5], row(prio), ALU.mult))
                    step(v.tensor_reduce(g1[:, 4], gb[:, 5], AX.X, ALU.max))
                    step(v.tensor_tensor(gb[:, hot], gb[:, 5], bc(4), ALU.is_equal))
                    if r == 0:
                        step(v.scalar_tensor_tensor(gb[:, 4], gb[:, 6], -2.0, gb[:, 3], ALU.mult, ALU.add))
                step(v.tensor_tensor(g1[:, 6], g1[:, 3], g1[:, 5], ALU.add))
                step(v.reciprocal(g1[:, 7], g1[:, 6]))
                step(v.tensor_tensor(gb[:, 6], gb[:, 6], gb[:, 5], ALU.add))
                step(v.tensor_tensor(gb[:, 6], gb[:, 6], gb[:, 3], ALU.mult))
                v.tensor_tensor(gb[:, 7], gb[:, 6], bc(7), ALU.mult).then_inc(gate_ready, 1)
                v.wait_ge(gate_ready, i + 1)
                assert n[0] == NCHAIN, n[0]

            def finish_chunk(i, n):
                v.wait_ge(yt_used, GT * i + 4 * n + 4 + 2)
                v.wait_ge(outs[n % 2], 16 * (GC // 2 * i + n // 2) + 16)
                v.tensor_tensor(fin[:, n % 2], x3[:, n], pf[:], ALU.add).then_inc(fin_ready, 1)

            with v.Fori(0, NGR) as i:
                for h in range(GC // 2):
                    for n in (2 * h, 2 * h + 1):
                        v.wait_ge(conv_done, GC * i + n + 1 + GC)
                        v.tensor_tensor(x3[:, n], X[:, bass.ds(i * GR + n * CH, CH)], pf[:], ALU.add).then_inc(s["src"], 1)
                    v.wait_ge(s["src"], GC * i + 2 * h + 3)
                    ln_vector(v, lambda j: x3[:, 2 * h + j], pm, d, sd, lambda j: z[:, 2 * h + j], s, (GC // 2) * i + h)
                gate(i)
                for t in range(GT):
                    v.wait_ge(lg_done, (GT + 1) * i + t + 2)
                    v.wait_ge(yt_used, GT * i + t + 1)
                    for m in range(NE):
                        k, e = m % 2, m // 2
                        src, ge = ex[:, 2 * (t % 2) + k, C * e:C * e + C], gb[:, 7, t, 4 * k + e:4 * k + e + 1]
                        if e == 0:
                            v.tensor_scalar(yt[:, t % 2, k], src, ge, None, ALU.mult).then_inc(mixed, 1)
                        else:
                            v.wait_ge(mixed, NE * (GT * i + t) + m - 1 + 2 * NE)
                            v.scalar_tensor_tensor(yt[:, t % 2, k], src, ge, yt[:, t % 2, k],
                                                   ALU.mult, ALU.add).then_inc(mixed, 1)
                    if t % 4 == 0 and t:
                        finish_chunk(i, t // 4 - 1)
                finish_chunk(i, GC - 1)


def layer_one(nc, I, S, out):
    with Arena(nc, "l1") as A:
        X = A.sb("x", [P, NB * T])
        cosp, ci = A.sb("cosp", [9, NB, C]), A.sb("ci", [P, NB])
        tokens_back(nc, I, S, X)
        with Arena(nc, "l1n") as B:
            XN = B.sb("xn", [P, NB * T])
            pool4 = B.sb("pool4", [P, NB * NCH * 32])
            second_norm(nc, I, X, XN, pool4)
            gates(nc, I, XN, pool4, cosp, ci)
            image(nc, S, XN, ci)
        experts(nc, I, S, X, cosp, out)


STAGES = (prepare, normalise_in, involution, forward, filters, spectrum, inverse, layer_one)


def tables():
    a, bl = np.arange(NA), np.arange(8)
    d1 = np.zeros((NA, 8, 2, 16, 8))
    th = 2 * np.pi * np.outer(a, np.arange(17)) / 32
    for k in bl:
        d1[:, k, 0, :, k] = np.cos(th[:, 0:16])
        d1[:, k, 1, 0, k] = np.cos(th[:, 16])
        d1[:, k, 1, 1:, k] = -np.sin(th[:, 1:16])
    b, f2 = np.arange(P), np.arange(NF2)
    fw = np.zeros((NF1, P, 2, 4, NF2))
    fi = np.zeros((NF1, NF2, 3, P))
    for f1 in range(NF1):
        f = f1 + 32 * f2
        for z in range(2):
            t = 2 * np.pi * (np.outer(b + z, f) % 4096) / 4096
            c, s = np.cos(t), np.sin(t)
            fw[f1, :, 0, 2 * z:2 * z + 2] = np.stack([c, -s], 1)
            if f1 not in (0, 16):
                fw[f1, :, 1, 2 * z:2 * z + 2] = np.stack([s, c], 1)
        t = 2 * np.pi * (np.outer(f, b) % 4096) / 4096
        w = (1.0 if f1 in (0, 16) else 2.0) / 4096
        fi[f1] = np.stack([np.cos(t), np.sin(t), -np.sin(t)], 1) * w
    d2 = np.zeros((32, 4, NA, 4))
    for k in range(4):
        d2[0:17, k, :, k] = np.cos(2 * np.pi * np.outer(np.arange(17), a) / 32)
        d2[17:, k, :, k] = -np.sin(2 * np.pi * np.outer(np.arange(1, 16), a) / 32)
    return {
        "ident": np.eye(P), "d1": d1.reshape(P, 2 * P), "fw": fw.reshape(NF1, P, 8 * NF2),
        "fi": fi.reshape(NF1, NF2, 3 * P), "d2": d2.reshape(P, 64), 
        "prio": np.tile(np.array([4.0, 3.0, 2.0, 1.0]), (P, 1)),
        "prio8": np.tile(np.arange(8.0, 0.0, -1.0), (P, 1)),
    }


def delta():
    d = np.zeros((T, 2), np.float32)
    d[0:2, 0] = 1.0
    d[2, 1] = 1.0
    return d


def layout(a):
    g = np.ascontiguousarray
    r = {
        "x": a["x"].reshape(NB, C, T), "w_reduce": a["L0_conv_w_reduce"], "b_reduce": a["L0_conv_b_reduce"].reshape(-1, 1),
        "w_span": a["L0_conv_w_span"].reshape(NG, TAPS, 32).transpose(2, 1, 0).reshape(32, -1),
        "b_span": a["L0_conv_b_span"].reshape(NG, TAPS).T.reshape(1, -1),
        "sigma": a["L0_ffn_sigma"], "phix": np.concatenate([a["L0_ffn_phi"], delta()], 1), "Mu": a["L0_ffn_M_u"], "Mpp": a["L0_ffn_M_phi_plus"],
        "Mpm": a["L0_ffn_M_phi_minus"], "lw": a["L0_ffn_log_weights"], "gum": a["L0_ffn_gumbel"],
        "W_sp": a["L1_conv_W_sp"], "b_sp": a["L1_conv_b_sp"].reshape(-1, 1), "W_o1": a["L1_conv_W_o1"],
        "b_o1": a["L1_conv_b_o1"].reshape(-1, 1), "W_o2": a["L1_conv_W_o2"], "b_o2": a["L1_conv_b_o2"],
        "W_i1": a["L1_conv_W_i1"], "b_i1": a["L1_conv_b_i1"].reshape(-1, 1), "W_i2": a["L1_conv_W_i2"],
        "b_i2": a["L1_conv_b_i2"].reshape(-1, 1), "router_w": a["L1_ffn_router_w"], "router_b": a["L1_ffn_router_b"],
        "expert_w": a["L1_ffn_expert_w"].transpose(1, 0, 2).reshape(C, NE * C), "expert_b": a["L1_ffn_expert_b"],
    }
    return {k: g(v) for k, v in r.items()}


def build(nc, I, out, stages):
    def dram(name, shape, dt=F32):
        return nc.dram_tensor(name, shape, dt).ap()

    S = {
        "XN": dram("s_xn", [NB, H, WP, C]), "XT": dram("s_xt", [NB * T, C]),
        "XNC": dram("s_xnc", [NB * NCH, C, CH]), "CV": dram("s_cv", [NB * T, C]),
        "X1C": dram("s_x1c", [NB, C, T]), "SF": dram("s_sf", [NB, 33, P, 2 * C]), "SP": dram("s_sp", [33, P, 2 * KX]),
        "WC": dram("s_wc", [P, TAPS * NG]), "KB": dram("s_kb", [1, TAPS * NG]), "D2M": dram("s_d2m", [P, 64]),
        "AS": dram("s_as", [2, 3, KX, C, C], BF16), "VP": dram("s_vp", [66, NB, 66]),
        "VS": dram("s_vs", [3, NF1, KX, 2, 2, NF2], BF16),
        "YD": dram("s_yd", [NF1, NF2, 16, C]), "TD": dram("s_td", [33, P, 2 * NB * C]),
    }
    for f in stages:
        f(nc, I, S, out) if f is layer_one else f(nc, I, S)


def kernel(**inputs):
    import concourse.bacc as bacc
    from concourse.bass_utils import run_bass_kernel_spmd

    nc = bacc.Bacc("TRN2", target_bir_lowering=False, num_devices=1)
    arrays, I = {}, {}
    for name, a in layout({k: np.asarray(v) for k, v in inputs.items()}).items():
        arrays[f"in_{name}"] = a
        I[name] = nc.dram_tensor(f"in_{name}", a.shape, mybir.dt.from_np(a.dtype), kind="ExternalInput").ap()
    for name, a in tables().items():
        a = a.astype(np.float32)
        arrays[f"table_{name}"] = a
        I[name] = nc.dram_tensor(f"table_{name}", a.shape, F32, kind="ExternalInput").ap()
    out = nc.dram_tensor("out", (NB, C, T), F32, kind="ExternalOutput").ap()
    build(nc, I, out, STAGES)
    r = run_bass_kernel_spmd(nc, [arrays], core_ids=[0])
    return r.results[0]["out"].reshape(NB, C, H, W)
```

```python
from contextlib import ExitStack

import numpy as np
import concourse.bass as bass
from concourse import mybir

F32 = mybir.dt.float32
BF16 = mybir.dt.bfloat16
ALU = mybir.AluOpType
ACT = mybir.ActivationFunctionType
AX = mybir.AxisListType

NB, C, H, W = 4, 128, 64, 64
T = H * W
P = 128
CH = 512
NCH = T // CH
NT = CH // P
KW, DIL, PADW, NG = 7, 2, 6, 8
TAPS = KW * KW
CG = C // NG
WP = W + 2 * PADW
RT = T // P
SLOTS = RT + KW - 1
NE = 8
KF = 16
KX = KF + 2
NF1, NF2, NA = 17, 128, 16
FT = 32
EPS_C, EPS_T = 1e-6, 1e-5


class Arena:

    def __init__(self, nc, tag):
        self.nc, self.tag, self.ctx = nc, tag, ExitStack()

    def __enter__(self):
        return self

    def __exit__(self, *a):
        return self.ctx.__exit__(*a)

    def sb(self, name, shape, dt=F32):
        return self.ctx.enter_context(self.nc.sbuf_tensor(f"{self.tag}_{name}", shape, dt))

    def ps(self, name, shape, dt=F32):
        return self.ctx.enter_context(self.nc.psum_tensor(f"{self.tag}_{name}", shape, dt))

    def sem(self, name):
        return self.ctx.enter_context(self.nc.semaphore(f"{self.tag}_{name}"))


def split3(eng, src, tmp, hi, mid, lo, step):
    step(eng.tensor_copy(hi, src))
    step(eng.tensor_tensor(tmp, src, hi, ALU.subtract))
    step(eng.tensor_copy(mid, tmp))
    step(eng.tensor_tensor(lo, tmp, mid, ALU.subtract))


def prepare(nc, I, S):
    with Arena(nc, "prep") as A:
        lg = A.sb("lg", [P, 2, 4])
        sm = A.sb("sm", [P, 12, 4])
        s1 = A.sb("s1", [P, 8])
        prio = A.sb("prio", [P, 4])
        sg = A.sb("sg", [P, 3, KF])
        wr = A.sb("wr", [32, C])
        br = A.sb("br", [32, 1])
        ws = A.sb("ws", [32, TAPS * NG])
        bs = A.sb("bs", [1, TAPS * NG])
        wc = A.sb("wc", [P, TAPS * NG])
        kb = A.sb("kb", [1, TAPS * NG])
        mp = A.sb("mp", [P, 2, 2, KF * C])
        mu = A.sb("mu", [P, 2, 3, C])
        acc = A.sb("acc", [P, 2, KF * C])
        au = A.sb("au", [P, 3, C])
        ab = A.sb("ab", [P, KX * C])
        tmp = A.sb("tmp", [P, KX * C])
        parts = A.sb("parts", [P, 3, KX * C], BF16)
        zero = A.sb("zero", [P, 2048])
        d2 = A.sb("d2", [P, 16, 4])
        mk = A.sb("mk", [P, 16])
        pw = A.ps("pw", [P, 512])
        pb = A.ps("pb", [1, 512])
        small_in = A.sem("small_in")
        mats_in = [A.sem(f"mats_in{k}") for k in range(2)]
        mats_used = A.sem("mats_used")
        wprod = A.sem("wprod")
        dve_done = A.sem("dve_done")
        act_done = A.sem("act_done")
        act_req = A.sem("act_req")
        wc_ready = A.sem("wc_ready")
        parts_ready = A.sem("parts_ready")
        parts_out = A.sem("parts_out")
        zero_ready = A.sem("zero_ready")
        out_done = A.sem("out_done")
        block = A.ctx.enter_context(nc.Block())

        @block.sync
        def _(sp):
            sp.dma_start(lg[:, 0, :], I["lw"].partition_broadcast(P)).then_inc(small_in, 16)
            sp.dma_start(lg[:, 1, :], I["gum"].partition_broadcast(P)).then_inc(small_in, 16)
            sp.dma_start(sg[:, 0, :], I["sigma"].partition_broadcast(P)).then_inc(small_in, 16)
            sp.dma_start(wr[:], I["w_reduce"]).then_inc(small_in, 16)
            sp.dma_start(br[:], I["b_reduce"]).then_inc(small_in, 16)
            sp.dma_start(ws[:], I["w_span"]).then_inc(small_in, 16)
            sp.dma_start(bs[:], I["b_span"]).then_inc(small_in, 16)
            sp.dma_start(prio[:], I["prio"]).then_inc(small_in, 16)
            sp.dma_start(d2[:], I["d2"].rearrange("p (a b) -> p a b", a=16)).then_inc(small_in, 16)
            for i in range(4):
                if i > 1:
                    sp.wait_ge(mats_used, i - 1)
                sp.dma_start(mp[:, i % 2, 0, :].rearrange("d (k e) -> d k e", k=KF),
                             I["Mpp"][i].rearrange("k d e -> d k e")).then_inc(mats_in[i % 2], 16)
                sp.dma_start(mp[:, i % 2, 1, :].rearrange("d (k e) -> d k e", k=KF),
                             I["Mpm"][i].rearrange("k d e -> d k e")).then_inc(mats_in[i % 2], 16)
                sp.dma_start(mu[:, i % 2], I["Mu"][i].rearrange("k d e -> d k e")).then_inc(mats_in[i % 2], 16)
            sp.wait_ge(zero_ready, 1)
            n = 0
            for b in range(NB):
                for side in (0, WP - PADW):
                    sp.dma_start(S["XN"][b][:, side:side + PADW, :], zero[0:H, 0:PADW * C].rearrange(
                        "h (w c) -> h w c", c=C)).then_inc(out_done, 16)
                    n += 1
            for b in range(NB):
                sp.dma_start(S["SF"][b, 32], zero[:, 0:256]).then_inc(out_done, 16)
                n += 1
            sp.dma_start(S["SP"][32], zero[:, 0:2 * KX]).then_inc(out_done, 16)
            sp.dma_start(S["VP"], zero[0:66, 0:NB * 66].rearrange("h (b w) -> h b w", b=NB)).then_inc(out_done, 16)
            sp.wait_ge(wc_ready, 3)
            sp.dma_start(S["WC"], wc[:]).then_inc(out_done, 16)
            sp.dma_start(S["KB"], kb[:]).then_inc(out_done, 16)
            sp.dma_start(S["D2M"], d2[:].rearrange("p a b -> p (a b)")).then_inc(out_done, 16)
            n += 5
            for x in range(2):
                sp.wait_ge(parts_ready, x + 1)
                for s in range(3):
                    sp.dma_start(S["AS"][x, s].rearrange("k d e -> d k e"), parts[:, s, :].rearrange(
                        "d (k e) -> d k e", k=KX)).then_inc(parts_out, 16)
            sp.wait_ge(parts_out, 96)
            sp.wait_ge(out_done, 16 * n)

        @block.tensor
        def _(pe):
            pe.wait_ge(small_in, 16 * 9)
            pe.matmul(pw[:, 0:TAPS * NG], wr[:], ws[:], start=True, stop=True).then_inc(wprod, 1)
            pe.matmul(pb[:, 0:TAPS * NG], br[:], ws[:], start=True, stop=True).then_inc(wprod, 1)

        @block.scalar
        def _(act):
            act.wait_ge(act_req, 1)
            act.activation(sm[:, 1, :], sm[:, 0, :], ACT.Exp).then_inc(act_done, 1)
            act.activation(sg[:, 1, :], sg[:, 0, :], ACT.Sqrt).then_inc(act_done, 1)
            act.wait_ge(act_done, 2)
            act.activation(sg[:, 2, :], sg[:, 1, :], ACT.Sqrt).then_inc(act_done, 1)

        @block.vector
        def _(v):
            n = [0]

            def step(ins):
                n[0] += 1
                ins.then_inc(dve_done, 1)
                v.wait_ge(dve_done, n[0])

            v.memset(zero[:], 0.0).then_inc(zero_ready, 1)
            v.wait_ge(small_in, 16 * 9)
            v.wait_ge(wprod, 2)
            v.tensor_copy(wc[:], pw[:, 0:TAPS * NG]).then_inc(wc_ready, 1)
            v.tensor_tensor(kb[:], pb[:, 0:TAPS * NG], bs[:], ALU.add).then_inc(wc_ready, 1)
            step(v.tensor_tensor(sm[:, 2, :], lg[:, 0, :], lg[:, 1, :], ALU.add))
            step(v.tensor_reduce(s1[:, 0:1], sm[:, 2, :], AX.X, ALU.max))
            v.tensor_scalar(sm[:, 0, :], sm[:, 2, :], s1[:, 0:1], None, ALU.subtract).then_inc(act_req, 1)
            v.wait_ge(act_done, 3)
            step(v.tensor_reduce(s1[:, 1:2], sm[:, 1, :], AX.X, ALU.add))
            step(v.reciprocal(s1[:, 2:3], s1[:, 1:2]))
            step(v.tensor_scalar(sm[:, 3, :], sm[:, 1, :], s1[:, 2:3], None, ALU.mult))
            step(v.tensor_reduce(s1[:, 3:4], sm[:, 3, :], AX.X, ALU.max))
            step(v.tensor_scalar(sm[:, 4, :], sm[:, 3, :], s1[:, 3:4], None, ALU.is_equal))
            step(v.tensor_tensor(sm[:, 5, :], sm[:, 4, :], prio[:], ALU.mult))
            step(v.tensor_reduce(s1[:, 4:5], sm[:, 5, :], AX.X, ALU.max))
            step(v.tensor_scalar(sm[:, 6, :], sm[:, 5, :], s1[:, 4:5], None, ALU.is_equal))
            step(v.tensor_tensor(sm[:, 7, :], sm[:, 6, :], sm[:, 3, :], ALU.subtract))
            step(v.tensor_tensor(sm[:, 8, :], sm[:, 7, :], sm[:, 3, :], ALU.add))
            step(v.memset(mk[:], 0.0))
            for i in range(4):
                step(v.tensor_scalar(mk[:, 0:16 >> i], mk[:, 0:16 >> i], sm[:, 6, i:i + 1], None, ALU.add))
            v.tensor_tensor(d2[:], d2[:], mk[:].rearrange("p (a o) -> p a o", o=1).to_broadcast([P, 16, 4]),
                            ALU.mult).then_inc(wc_ready, 1)
            for i in range(4):
                v.wait_ge(mats_in[i % 2], 48 * (i // 2 + 1))
                wi = sm[:, 8, i:i + 1]
                for dst, src in ((acc, mp[:, i % 2]), (au, mu[:, i % 2])):
                    if i == 0:
                        last = v.tensor_scalar(dst[:], src, wi, None, ALU.mult)
                    else:
                        last = v.scalar_tensor_tensor(dst[:], src, wi, dst[:], ALU.mult, ALU.add)
                    step(last)
                v.sem_inc(mats_used, 1)
            sv = sg[:, 2, :].rearrange("p (k o) -> p k o", o=1).to_broadcast([P, KF, C])
            for x, (op, m) in enumerate(((ALU.add, 0), (ALU.subtract, 1))):
                step(v.tensor_tensor(tmp[:, 0:KF * C], acc[:, 0, :], acc[:, 1, :], op))
                step(v.tensor_tensor(ab[:, 0:KF * C].rearrange("p (k e) -> p k e", k=KF),
                                     tmp[:, 0:KF * C].rearrange("p (k e) -> p k e", k=KF), sv, ALU.mult))
                step(v.tensor_copy(ab[:, KF * C:KF * C + C], au[:, m, :]))
                step(v.tensor_copy(ab[:, KF * C + C:], au[:, 2, :]))
                if x:
                    v.wait_ge(parts_out, 48)
                split3(v, ab[:], tmp[:], parts[:, 0, :], parts[:, 1, :], parts[:, 2, :], step)
                v.sem_inc(parts_ready, 1)



def normalise_in(nc, I, S):
    NQ, D = NB * NCH, 4
    with Arena(nc, "lnc") as A:
        ident = A.sb("ident", [P, P])
        eps = A.sb("eps", [P, 1])
        xc = A.sb("xc", [P, D, CH])
        xt = A.sb("xt", [P, D, NT, C])
        xn = A.sb("xn", [P, D, NT, C])
        xnc = A.sb("xnc", [P, D, CH])
        st = A.sb("st", [P, D, NT, 6])
        mv = A.sb("mv", [P, D, NT, 2])
        sd = A.sb("sd", [P, D, NT])
        rs = A.sb("rs", [P, D, NT])
        nm = A.sb("nm", [P, D, NT])
        px = A.ps("px", [P, D, CH])
        pn = A.ps("pn", [P, D, CH])
        const_in = A.sem("const_in")
        x_in = [A.sem(f"x_in{k}") for k in range(D)]
        outs = [A.sem(f"outs{k}") for k in range(D)]
        x_turned, xt_ready, st_ready = A.sem("x_turned"), A.sem("xt_ready"), A.sem("st_ready")
        mv_ready, sd_ready, rs_ready = A.sem("mv_ready"), A.sem("sd_ready"), A.sem("rs_ready")
        nm_ready, xn_ready, xn_turned = A.sem("nm_ready"), A.sem("xn_ready"), A.sem("xn_turned")
        xnc_ready, eps_ready = A.sem("xnc_ready"), A.sem("eps_ready")
        passed = A.sem("passed")
        block = A.ctx.enter_context(nc.Block())
        xv = I["x"].rearrange("b c (n m) -> b n c m", m=CH)

        @block.gpsimd
        def _(pool):
            pool.memset(eps[:], EPS_C).then_inc(eps_ready, 1)
            with pool.Fori(0, NQ // D) as i:
                for k in range(D):
                    q = D * i + k
                    pool.wait_ge(x_turned, q + 1)
                    pool.dma_start(xc[:, k, :], xv[bass.ds(q // NCH, 1), bass.ds(q % NCH, 1)].rearrange(
                        "o a c m -> (o a c) m")).then_inc(x_in[k], 16)

        @block.sync
        def _(sp):
            sp.dma_start(ident[:], I["ident"]).then_inc(const_in, 16)
            rows = S["XN"].rearrange("b (n t r) w c -> b n r w t c", t=NT, r=2)
            with sp.Fori(0, NQ // D) as i:
                for k in range(D):
                    q = D * i + k
                    sp.wait_ge(xn_ready, q + 1)
                    sp.dma_start(S["XT"].rearrange("(q t p) c -> q p t c", p=P, t=NT)[bass.ds(q, 1)].rearrange(
                        "o p t c -> (o p) t c"), xt[:, k]).then_inc(outs[k], 16)
                    for r in range(2):
                        sp.dma_start(rows[bass.ds(q // NCH, 1), bass.ds(q % NCH, 1), r, PADW:PADW + W].rearrange(
                            "o a w t c -> (o a w) t c"), xn[64 * r:64 * r + 64, k]).then_inc(outs[k], 16)
                    sp.wait_ge(xnc_ready, q + 1 + D)
                    sp.dma_start(S["XNC"][bass.ds(q, 1)].rearrange("o c m -> (o c) m"),
                                 xnc[:, k]).then_inc(outs[k], 16)
            for k in range(D):
                sp.wait_ge(outs[k], 64 * (NQ // D) + 64)

        @block.tensor
        def _(pe):
            pe.wait_ge(const_in, 16)
            with pe.Fori(0, NQ // D) as i:
                for k in range(D):
                    pe.wait_ge(x_in[k], 16 * i + 16)
                    pe.wait_ge(xt_ready, D * i + k + 1)
                    for t in range(NT):
                        m = pe.transpose(px[:, k, t * P:(t + 1) * P], xc[:, k, t * P:(t + 1) * P], ident[:])
                    m.then_inc(x_turned, 1)
                for k in range(D):
                    pe.wait_ge(xn_ready, D * i + k + 1)
                    pe.wait_ge(xnc_ready, D * i + k + 1)
                    for t in range(NT):
                        m = pe.transpose(pn[:, k, t * P:(t + 1) * P], xn[:, k, t, :], ident[:])
                    m.then_inc(xn_turned, 1)

        @block.scalar
        def _(act):
            act.sem_inc(x_turned, D)
            act.sem_inc(xt_ready, D)
            act.sem_inc(xnc_ready, D)
            for k in range(D):
                act.sem_inc(outs[k], 64)
            act.wait_ge(eps_ready, 1)
            with act.Fori(0, NQ // D) as i:
                for k in range(D):
                    act.wait_ge(x_turned, D * i + k + 1 + D)
                    act.wait_ge(outs[k], 64 * i + 64)
                    act.activation(xt[:, k], px[:, k].rearrange("p (t c) -> p t c", t=NT), ACT.Copy).then_inc(xt_ready, 1)
                for k in range(D):
                    act.wait_ge(mv_ready, D * i + k + 1)
                    act.activation(sd[:, k], mv[:, k, :, 1], ACT.Sqrt, bias=eps[:]).then_inc(sd_ready, 1)
                for k in range(D):
                    act.wait_ge(nm_ready, D * i + k + 1)
                    act.wait_ge(xt_ready, D * i + k + 1 + D)
                    for t in range(NT):
                        m = act.activation(xn[:, k, t, :], xt[:, k, t, :], ACT.Identity,
                                           bias=nm[:, k, t:t + 1], scale=rs[:, k, t:t + 1])
                    m.then_inc(xn_ready, 1)
                for k in range(D):
                    act.wait_ge(xn_turned, D * i + k + 1)
                    act.activation(xnc[:, k], pn[:, k], ACT.Copy).then_inc(xnc_ready, 1)

        @block.vector
        def _(v):
            with v.Fori(0, NQ // D) as i:
                for k in range(D):
                    v.wait_ge(xt_ready, D * i + k + 1 + D)
                    for t in range(NT):
                        m = v.bn_stats(st[:, k, t, :], xt[:, k, t, :])
                    m.then_inc(st_ready, 1)
                for k in range(D):
                    v.wait_ge(st_ready, D * i + k + 1)
                    v.sem_inc(passed, 1)
                    for t in range(NT):
                        m = v.bn_aggr(mv[:, k, t, :], st[:, k, t, :])
                    m.then_inc(mv_ready, 1)
                for k in range(D):
                    v.wait_ge(sd_ready, D * i + k + 1)
                    v.reciprocal(rs[:, k], sd[:, k]).then_inc(rs_ready, 1)
                for k in range(D):
                    v.wait_ge(rs_ready, D * i + k + 1)
                    v.scalar_tensor_tensor(nm[:, k], mv[:, k, :, 0], -1.0, rs[:, k],
                                           ALU.mult, ALU.mult).then_inc(nm_ready, 1)


NPAIR = 23
ITEMS = (["s"] + ["p"] * 8) * 3
ITEMS.pop()
PR = 14
SR = 4
HT = 25


def involution(nc, I, S):
    items, t = [], 0
    for it in ITEMS:
        items.append((t,) if it == "s" else (t, t + 1))
        t += len(items[-1])
    assert t == TAPS
    pairs = [k for k, tt in enumerate(items) if len(tt) == 2]
    NI, NQ = len(items) + 1, NB * NCH
    pe_upto = [2 + max(k for k, tt in enumerate(items) if len(tt) == 1 and tt[0] < 7 * (g + 1)) for g in range(7)]
    pool_upto = [sum(items[k][0] < 7 * (g + 1) for k in pairs) for g in range(7)]
    M0 = TAPS * 8
    with Arena(nc, "inv") as A:
        ident = A.sb("ident", [P, P])
        wc = A.sb("wc", [P, TAPS * NG])
        kb = A.sb("kb", [1, TAPS * NG])
        ones = A.sb("ones", [1, P])
        xnc = A.sb("xnc", [P, 2, CH])
        X7 = A.sb("X7", [P, KW, SLOTS * C])
        prod = A.sb("prod", [P, PR, CH])
        psm = A.sb("psm", [P, SR, CH])
        xt = A.sb("xt", [P, 2, CH])
        cv = A.sb("cv", [P, 2, CH])
        ker = A.ps("ker", [P, 2, NT, 256])
        acc = A.ps("acc", [P, 2, CH])
        const_in, ones_ready, pads_ready = A.sem("const_in"), A.sem("ones_ready"), A.sem("pads_ready")
        xnc_in = [A.sem(f"xnc_in{k}") for k in range(2)]
        xt_in = [A.sem(f"xt_in{k}") for k in range(2)]
        x7_in = [A.sem(f"x7_in{k}") for k in range(4)]
        ker_ready, mul_done, pair_done = A.sem("ker_ready"), A.sem("mul_done"), A.sem("pair_done")
        item_done, cv_ready = A.sem("item_done"), A.sem("cv_ready")
        cv_out = [A.sem(f"cv_out{k}") for k in range(2)]
        block = A.ctx.enter_context(nc.Block())
        G7 = 16 * 2 * KW

        def slot(c, tap):
            return 7 * ((7 * c + tap // 7) % 2) + tap % 7

        @block.sync
        def _(sp):
            for d, s in ((ident, I["ident"]), (wc, S["WC"]), (kb, S["KB"])):
                sp.dma_start(d[:], s).then_inc(const_in, 16)
            rows = S["XN"].rearrange("b (n t r) w c -> b n r w t c", t=NT, r=2)
            with sp.Fori(0, NQ // 4) as i:
                for c in range(4):
                    q = 4 * i + c
                    sp.wait_ge(mul_done, TAPS * (q + 2))
                    sp.wait_ge(x7_in[c], G7 * i + G7)
                    for j in range(KW):
                        for r in range(2):
                            dst = X7[64 * r:64 * r + 64, j, bass.ds((i % 2) * (16 * C) + (3 + 4 * c) * C, CH)]
                            sp.dma_start(dst.rearrange("p (t c) -> p t c", t=NT),
                                         rows[bass.ds(i // 2, 1), bass.ds((i % 2) * 4 + c, 1), r,
                                              DIL * j:DIL * j + W].rearrange("o a w t c -> (o a w) t c")
                                         ).then_inc(x7_in[c], 16)
            sp.wait_ge(x7_in[0], G7 * (NQ // 4) + G7)
            sp.sem_inc(x7_in[0], G7)

        @block.gpsimd
        def _(pool):
            for s0 in (0, SLOTS - 3):
                m = pool.memset(X7[:, :, s0 * C:(s0 + 3) * C], 0.0)
                m.then_inc(pads_ready, 1)
            pool.memset(ones[:], 1.0).then_inc(ones_ready, 1)
            pool.sem_inc(pair_done, NPAIR)
            with pool.Fori(0, NQ // 4) as i:
                for c in range(4):
                    q = 4 * i + c
                    for p, k in enumerate(pairs):
                        t0, t1 = items[k]
                        pool.wait_ge(mul_done, M0 + TAPS * q + t1 + 1)
                        old = pairs[p - SR if p >= SR else (NPAIR - 1 - p) // SR * SR + p]
                        pool.wait_ge(item_done, NI * q + old + 2 + (NI if p >= SR else 0))
                        pool.tensor_tensor(psm[:, p % SR, :], prod[:, slot(c, t0), :], prod[:, slot(c, t1), :],
                                           ALU.add).then_inc(pair_done, 1)

        @block.tensor
        def _(pe):
            pe.wait_ge(const_in, 48)
            pe.wait_ge(ones_ready, 1)

            def kernels(k, half):
                lo, hi = (0, HT * NG) if half == 0 else (HT * NG, TAPS * NG)
                for t in range(NT):
                    o = ker[:, half, t, 0:hi - lo]
                    pe.matmul(o, xnc[:, k, t * P:(t + 1) * P], wc[:, lo:hi], start=True, stop=False)
                    m = pe.matmul(o, ones[:], kb[:, lo:hi], start=False, stop=True)
                m.then_inc(ker_ready, 1)

            pe.wait_ge(xnc_in[0], 16)
            kernels(0, 0)
            with pe.Fori(0, NQ // 4) as i:
                for c in range(4):
                    q = 4 * i + c
                    pe.wait_ge(mul_done, M0 + TAPS * q)
                    kernels(c % 2, 1)
                    pe.wait_ge(cv_ready, q + 1)
                    pe.wait_ge(xt_in[c % 2], 16 * (2 * i + c // 2) + 16)
                    pe.matmul(acc[:, c % 2, :], ident[:], xt[:, c % 2, :], start=True, stop=False).then_inc(item_done, 1)
                    for k, tt in enumerate(items):
                        if k == 14:
                            pe.wait_ge(mul_done, M0 + TAPS * q + HT)
                            pe.wait_ge(xnc_in[(c + 1) % 2], 16 * ((4 * i + c + 1) // 2) + 16)
                            kernels((c + 1) % 2, 0)
                        if len(tt) == 1:
                            pe.wait_ge(mul_done, M0 + TAPS * q + tt[0] + 1)
                            src = prod[:, slot(c, tt[0]), :]
                        else:
                            p = pairs.index(k)
                            pe.wait_ge(pair_done, NPAIR * q + NPAIR + p + 1)
                            src = psm[:, p % SR, :]
                        pe.matmul(acc[:, c % 2, :], ident[:], src, start=False,
                                  stop=(k == len(items) - 1)).then_inc(item_done, 1)

        @block.scalar
        def _(act):
            act.sem_inc(cv_ready, 2)
            act.sem_inc(item_done, NI)
            act.sem_inc(ker_ready, 1)
            for k in range(4):
                act.sem_inc(x7_in[k], G7)
            for k in range(2):
                act.sem_inc(cv_out[k], 16)

            def load(q, k):
                act.dma_start(xnc[:, k], q).then_inc(xnc_in[k], 16)

            xq = S["XNC"]
            tiles = "(q t p) c -> q p t c"

            def load_xt(q, k):
                src = S["XT"].rearrange(tiles, p=P, t=NT)
                src = src[q] if isinstance(q, int) else src[bass.ds(q, 1)].rearrange("o p t c -> (o p) t c")
                act.dma_start(xt[:, k].rearrange("p (t c) -> p t c", t=NT), src).then_inc(xt_in[k], 16)

            load(xq[0], 0)
            load(xq[1], 1)
            load_xt(0, 0)
            load_xt(1, 1)
            with act.Fori(0, NQ // 4) as i:
                for c in range(4):
                    q, k = 4 * i + c, c % 2
                    act.wait_ge(ker_ready, 2 * q + 3)
                    load(xq[bass.ds((q + 2) % NQ, 1)].rearrange("o c m -> (o c) m"), k)
                    act.wait_ge(item_done, NI * q + 2 * NI)
                    load_xt((q + 2) % NQ, k)
                    act.wait_ge(cv_out[k], 16 * (2 * i + c // 2) + 16)
                    act.activation(cv[:, k], acc[:, k], ACT.Copy).then_inc(cv_ready, 1)
                    act.wait_ge(cv_ready, q + 3)
                    act.dma_start(S["X1"].rearrange("(q t p) c -> q p t c", p=P, t=NT)[bass.ds(q, 1)].rearrange(
                        "o p t c -> (o p) t c"), cv[:, k].rearrange("p (t c) -> p t c", t=NT)).then_inc(cv_out[k], 16)
            for k in range(2):
                act.wait_ge(cv_out[k], 16 * (NQ // 2) + 16)
                act.wait_ge(xnc_in[k], 16 * (NQ // 2 + 1))
                act.wait_ge(xt_in[k], 16 * (NQ // 2 + 1))

        @block.vector
        def _(v):
            v.sem_inc(mul_done, M0)
            v.wait_ge(pads_ready, 2)
            with v.Fori(0, NQ // 4) as i:
                for c in range(4):
                    q = 4 * i + c
                    v.wait_ge(x7_in[c], G7 * i + 2 * G7)
                    if c < 3:
                        v.wait_ge(x7_in[c + 1], G7 * i + 2 * G7)
                    else:
                        v.wait_ge(x7_in[0], G7 * i + 3 * G7)
                    for tap in range(TAPS):
                        if tap % 7 == 0:
                            g = tap // 7
                            back = 0 if g >= 2 else 1
                            o = (g - 2) % 7
                            v.wait_ge(item_done, NI * q + pe_upto[o] + NI * (1 - back))
                            v.wait_ge(pair_done, NPAIR * q + pool_upto[o] + NPAIR * (1 - back))
                        if tap in (0, HT):
                            v.wait_ge(ker_ready, 2 * q + 2 + (tap > 0))
                        ti, tj = divmod(tap, KW)
                        h, w = (0, tap) if tap < HT else (1, tap - HT)
                        kv = ker[:, h, :, w * NG:(w + 1) * NG].rearrange("p t (g o) -> p t g o", o=1)
                        xv = X7[:, tj, bass.ds((i % 2) * (16 * C) + (4 * c + ti) * C, CH)]
                        v.tensor_tensor(prod[:, slot(c, tap), :].rearrange("p (t g c) -> p t g c", t=NT, g=NG),
                                        kv.to_broadcast([P, NT, NG, CG]),
                                        xv.rearrange("p (t g c) -> p t g c", t=NT, g=NG),
                                        ALU.mult).then_inc(mul_done, 1)


HH = 8


def forward(nc, I, S):
    NU = NB * 2
    with Arena(nc, "fwd") as A:
        ident = A.sb("ident", [P, P])
        d1 = A.sb("d1", [P, 2 * P])
        eps = A.sb("eps", [P, 1])
        xt = A.sb("xt", [P, 2, HH, 2, C])
        u = A.sb("u", [P, 2, HH, 2, C])
        ph = A.sb("ph", [P, 16, 2 * KX])
        x1c = A.sb("x1c", [P, 2, T])
        so = A.sb("so", [P, 2, 2, HH, 2 * C])
        po = A.sb("po", [P, 2, 16, 2 * KX])
        st = A.sb("st", [P, 2, 16, 6])
        mv = A.sb("mv", [P, 2, 16, 2])
        sd = A.sb("sd", [P, 2, 16])
        rs = A.sb("rs", [P, 2, 16])
        nm = A.sb("nm", [P, 2, 16])
        pt = A.ps("pt", [P, 4, CH])
        pf = A.ps("pf", [P, 4, CH])
        const_in, eps_ready = A.sem("const_in"), A.sem("eps_ready")
        x_in = [A.sem(f"x_in{k}") for k in range(2)]
        st_ready, mv_ready = A.sem("st_ready"), A.sem("mv_ready")
        sd_ready, rs_ready, nm_ready = A.sem("sd_ready"), A.sem("rs_ready"), A.sem("nm_ready")
        u_ready, turned, x1c_ready = A.sem("u_ready"), A.sem("turned"), A.sem("x1c_ready")
        f_done, so_ready, so_a = A.sem("f_done"), A.sem("so_ready"), A.sem("so_a")
        s_out = [[A.sem(f"s_out{half}{k}") for k in range(2)] for half in range(2)]
        c_out = A.sem("c_out")
        passed = A.sem("passed")
        block = A.ctx.enter_context(nc.Block())
        tok = "(b q k h p) c -> b k q (h p c)"

        @block.gpsimd
        def _(pool):
            pool.memset(eps[:], EPS_T).then_inc(eps_ready, 1)

        @block.sync
        def _(sp):
            sp.dma_start(ident[:], I["ident"]).then_inc(const_in, 16)
            sp.dma_start(d1[:], I["d1"]).then_inc(const_in, 16)
            sp.dma_start(ph[:], I["phix"].rearrange("(q h p) k -> q h (p k)", q=P, h=16)).then_inc(const_in, 16)
            with sp.Fori(0, NU // 2) as i:
                for k in range(2):
                    sp.wait_ge(turned, 4 * (2 * i + k) + 4)
                    sp.sem_inc(passed, 1)
                    sp.wait_ge(u_ready, 2 * i + k + 1)
                    v = S["X1"].rearrange(tok, b=NB, q=P, k=2, h=HH)
                    sp.dma_start(xt[:, k].rearrange("p i q c -> p (i q c)"), v[bass.ds(i, 1), k].rearrange(
                        "o q m -> (o q) m")).then_inc(x_in[k], 16)

        def units(eng, body):
            with eng.Fori(0, NU // 2 - 1) as i:
                for k in range(2):
                    body(2 * i + k, k, True, i)
            for k in range(2):
                body(NU - 2 + k, k, k == 0, NU // 2 - 1)

        @block.vector
        def _(v):
            def statistics(n, k, i):
                v.wait_ge(x_in[k], 16 * i + 16)
                for t in range(16):
                    m = v.bn_stats(st[:, k, t, :], xt[:, k, t // 2, t % 2, :])
                m.then_inc(st_ready, 1)
                v.wait_ge(st_ready, n + 1)
                v.sem_inc(passed, 1)
                for t in range(16):
                    m = v.bn_aggr(mv[:, k, t, :], st[:, k, t, :])
                m.then_inc(mv_ready, 1)
                v.wait_ge(sd_ready, n + 1)
                v.reciprocal(rs[:, k], sd[:, k]).then_inc(rs_ready, 1)
                v.wait_ge(rs_ready, n + 1)
                v.scalar_tensor_tensor(nm[:, k], mv[:, k, :, 0], -1.0, rs[:, k], ALU.mult, ALU.mult).then_inc(nm_ready, 1)

            def body(n, k, more, i):
                if more:
                    v.wait_ge(u_ready, n + 2)
                    statistics(n + 1, 1 - k, i + k)
                v.wait_ge(s_out[1][k], 16 * i + 16)
                for c in range(4):
                    v.wait_ge(f_done, 8 * n + 2 * c + 2)
                    v.tensor_copy(so[:, 1, k, 2 * c:2 * c + 2, :].rearrange("p h m -> p (h m)"),
                                  pf[:, 2 * (c % 2) + 1, :]).then_inc(so_ready, 1)

            statistics(0, 0, 0)
            units(v, body)
            for n in range(2):
                v.wait_ge(f_done, 8 * NU + 2 * n + 2)
                v.tensor_copy(po[:, 1, 8 * n:8 * n + 8, :].rearrange("p h m -> p (h m)"),
                              pf[:, 2 * n + 1, 0:16 * KX]).then_inc(so_ready, 1)

        @block.scalar
        def _(act):
            act.sem_inc(turned, 8)
            act.sem_inc(x1c_ready, 4)
            act.sem_inc(u_ready, 2)
            act.sem_inc(so_ready, 2)
            act.sem_inc(so_a, 2)
            for half in range(2):
                for k in range(2):
                    act.sem_inc(s_out[half][k], 16)
            act.sem_inc(c_out, 16)
            act.wait_ge(eps_ready, 1)

            def normalise(n, k):
                act.wait_ge(mv_ready, n + 1)
                act.activation(sd[:, k], mv[:, k, :, 1], ACT.Sqrt, bias=eps[:]).then_inc(sd_ready, 1)
                act.wait_ge(nm_ready, n + 1)
                for t in range(16):
                    m = act.activation(u[:, k, t // 2, t % 2, :], xt[:, k, t // 2, t % 2, :], ACT.Identity,
                                       bias=nm[:, k, t:t + 1], scale=rs[:, k, t:t + 1])
                m.then_inc(u_ready, 1)

            def body(n, k, more, i):
                if k == 0:
                    act.wait_ge(c_out, 16 * i + 16)
                for c in range(4):
                    act.wait_ge(turned, 4 * n + c + 9)
                    dst = x1c[:, 0, :].rearrange("c (q m) -> c m q", q=P)[:, 16 * k + 4 * c:16 * k + 4 * c + 4]
                    act.activation(dst, pt[:, c, :].rearrange("c (m q) -> c m q", m=4),
                                   ACT.Copy).then_inc(x1c_ready, 1)
                if more:
                    normalise(n + 1, 1 - k)
                act.wait_ge(s_out[0][k], 16 * i + 16)
                for c in range(4):
                    act.wait_ge(f_done, 8 * n + 2 * c + 1)
                    act.activation(so[:, 0, k, 2 * c:2 * c + 2, :].rearrange("p h m -> p (h m)"),
                                   pf[:, 2 * (c % 2), :], ACT.Copy).then_inc(so_a, 1)
                for half, ready in ((0, so_a), (1, so_ready)):
                    act.wait_ge(ready, 4 * n + 6)
                    dst = S["SF"][:, 16 * half:16 * half + 16].rearrange("b f (l y h) m -> b y (f l) (h m)", y=2, l=8)
                    dst = dst[i, k] if isinstance(i, int) else dst[bass.ds(i, 1), k].rearrange("o q m -> (o q) m")
                    act.dma_start(dst, so[:, half, k].rearrange("p h m -> p (h m)")).then_inc(
                        s_out[half][k], 16)
                if k == 1:
                    act.wait_ge(x1c_ready, 4 * n + 8)
                    dst = S["X1C"][i] if isinstance(i, int) else S["X1C"][bass.ds(i, 1)].rearrange("o c t -> (o c) t")
                    act.dma_start(dst, x1c[:, 0, :]).then_inc(c_out, 16)

            normalise(0, 0)
            units(act, body)
            for n in range(2):
                act.wait_ge(f_done, 8 * NU + 2 * n + 1)
                act.activation(po[:, 0, 8 * n:8 * n + 8, :].rearrange("p h m -> p (h m)"),
                               pf[:, 2 * n, 0:16 * KX], ACT.Copy).then_inc(so_a, 1)
            for half, ready in ((0, so_a), (1, so_ready)):
                act.wait_ge(ready, 4 * NU + 4)
                act.dma_start(S["SP"][16 * half:16 * half + 16].rearrange("f (l h) m -> (f l) (h m)", l=8),
                              po[:, half].rearrange("p h m -> p (h m)")).then_inc(
                                  s_out[half][0], 16)
            act.wait_ge(c_out, 16 * NB + 16)
            for half in range(2):
                act.wait_ge(s_out[half][0], 16 * (NU // 2) + 16 + 16)
                act.wait_ge(s_out[half][1], 16 * (NU // 2) + 16)

        @block.tensor
        def _(pe):
            pe.wait_ge(const_in, 48)

            def turn(n, k, i):
                pe.wait_ge(x_in[k], 16 * i + 16)
                for c in range(4):
                    pe.wait_ge(x1c_ready, 4 * n + c + 1)
                    for m4 in range(4):
                        m = pe.transpose(pt[:, c, m4 * P:m4 * P + P],
                                         xt[:, k, 2 * c + m4 // 2, m4 % 2, :], ident[:])
                    m.then_inc(turned, 1)

            def body(n, k, more, i):
                pe.wait_ge(u_ready, n + 3)
                for c in range(4):
                    for half, free in ((0, so_a), (1, so_ready)):
                        pe.wait_ge(free, 4 * n + c + 1)
                        pe.matmul(pf[:, 2 * (c % 2) + half, :], d1[:, half * P:half * P + P],
                                  u[:, k, 2 * c:2 * c + 2].rearrange("p h q c -> p (h q c)"),
                                  start=True, stop=True).then_inc(f_done, 1)
                if more:
                    turn(n + 1, 1 - k, i + k)

            turn(0, 0, 0)
            units(pe, body)
            for n in range(2):
                for half, free in ((0, so_a), (1, so_ready)):
                    pe.wait_ge(free, 4 * NU + n + 1)
                    pe.matmul(pf[:, 2 * n + half, 0:16 * KX], d1[:, half * P:half * P + P],
                              ph[:, 8 * n:8 * n + 8, :].rearrange("p h m -> p (h m)"),
                              start=True, stop=True).then_inc(f_done, 1)


def filters(nc, I, S):
    with Arena(nc, "flt") as A:
        sp_ = A.sb("sp", [P, 2, 2, 2 * KX])
        fw = A.sb("fw", [P, 2, 2, 2, NF2])
        vv = A.sb("vv", [KX, 2, 2 * NF2])
        tmp = A.sb("tmp", [KX, 2, 2 * NF2])
        parts = A.sb("parts", [KX, 2, 3, 2, 2 * NF2], BF16)
        pv = A.ps("pv", [KX, 2, 2, 256])
        loads = [A.sem(f"loads{k}") for k in range(2)]
        outs = [A.sem(f"outs{k}") for k in range(2)]
        v_done, chain, parts_ready = A.sem("v_done"), A.sem("chain"), A.sem("parts_ready")
        block = A.ctx.enter_context(nc.Block())
        spx = S["SP"]

        @block.sync
        def _(sp):
            for f in range(NF1):
                k = f % 2
                if f >= 2:
                    sp.wait_ge(v_done, f - 1)
                sp.dma_start(sp_[:, k, 0], spx[f]).then_inc(loads[k], 16)
                sp.dma_start(sp_[:, k, 1], spx[16 + f]).then_inc(loads[k], 16)
                sp.dma_start(fw[:, k], I["fw"][f].rearrange("b (p s f) -> b p s f", p=2, s=4)[:, :, 0:2]).then_inc(loads[k], 16)

        @block.tensor
        def _(pe):
            for f in range(NF1):
                k = f % 2
                pe.wait_ge(loads[k], 48 * (f // 2) + 48)
                if f >= 2:
                    pe.wait_ge(chain, 4 * (f - 1))
                for x in range(2):
                    for part in range(2):
                        m = pe.matmul(pv[:, k, x], sp_[:, k, part, x * KX:x * KX + KX],
                                      fw[:, k, part].rearrange("b s f -> b (s f)"), start=part == 0, stop=part == 1)
                m.then_inc(v_done, 1)

        @block.vector
        def _(v):
            n = [0]

            def step(ins):
                n[0] += 1
                ins.then_inc(chain, 1)
                v.wait_ge(chain, n[0])

            for f in range(NF1):
                k = f % 2
                v.wait_ge(v_done, f + 1)
                if f >= 2:
                    v.wait_ge(outs[k], 48 * (f // 2))
                split3(v, pv[:, k], tmp[:], parts[:, k, 0], parts[:, k, 1], parts[:, k, 2], step)
                v.sem_inc(parts_ready, 1)

        @block.scalar
        def _(act):
            for f in range(NF1):
                k = f % 2
                act.wait_ge(parts_ready, f + 1)
                for s in range(3):
                    act.dma_start(S["VS"][s, f].rearrange("k x c f -> k x (c f)"), parts[:, k, s]).then_inc(outs[k], 16)
            for k in range(2):
                act.wait_ge(outs[k], 48 * ((NF1 + 1 - k) // 2))


V_PARTS, A_PARTS = (0, 0, 1, 0, 1, 2), (0, 1, 0, 2, 1, 0)
KROWS = KX * len(V_PARTS)


def spectrum(nc, I, S):
    NTL = NF2 // FT
    UF = 12 * NB
    with Arena(nc, "spc") as A:
        AS = A.sb("as", [KROWS, 2, C, C], BF16)
        V = A.sb("v", [KROWS, 2, 2, 2, NF2], BF16)
        G = A.sb("g", [P, FT, 4, C])
        U = A.sb("u", [P, 2, NF2 * UF + 32])
        Ss = A.sb("s", [P, 2, 2, NB, 2 * C])
        F = A.sb("f", [P, 2, 2, 4, NF2])
        yo = A.sb("yo", [P, 8, C])
        pg = A.ps("pg", [P, 4, 512])
        pu = A.ps("pu", [P, 2, 512])
        py = A.ps("py", [P, 2, 4, C])
        as_in = A.sem("as_in")
        in_v = [A.sem(f"in_v{k}") for k in range(2)]
        in_s = [A.sem(f"in_s{k}") for k in range(2)]
        u_done, u_ready = A.sem("u_done"), A.sem("u_ready")
        g_done, ga, gd = A.sem("g_done"), A.sem("ga"), A.sem("gd")
        y_done, ya, yd = A.sem("y_done"), A.sem("ya"), A.sem("yd")
        y_out, pad_ready = A.sem("y_out"), A.sem("pad_ready")
        block = A.ctx.enter_context(nc.Block())

        def one(ap, i):
            if isinstance(i, int):
                return ap[i]
            n = len(ap.shape)
            names = [f"x{k}" for k in range(n)]
            return ap[bass.ds(i, 1)].rearrange(f"{' '.join(names)} -> ({names[0]} {names[1]}) {' '.join(names[2:])}")

        @block.gpsimd
        def _(sp):
            for g, part in enumerate(A_PARTS):
                for x in range(2):
                    sp.dma_start(AS[KX * g:KX * g + KX, x].rearrange("k e d -> k (e d)"),
                                 S["AS"][x, part].rearrange("k d e -> k (d e)")).then_inc(as_in, 16)

            def load(f, k):
                for g, part in enumerate(V_PARTS):
                    sp.dma_start(V[KX * g:KX * g + KX, k].rearrange("k x c f -> k (x c f)"),
                                 one(S["VS"][part], f).rearrange("k x c f -> k (x c f)")).then_inc(in_v[k], 16)
                sp.dma_start(F[:, k].rearrange("b p s f -> b (p s f)"), one(I["fw"], f)).then_inc(in_s[k], 16)
                for part in range(2):
                    src = S["SF"].rearrange("n f b m -> f b n m")
                    sp.dma_start(Ss[:, k, part], one(src, f + 16 * part)).then_inc(in_s[k], 16)

            load(0, 0)
            load(1, 1)
            with sp.Fori(0, NF1 // 2) as i:
                for k in range(2):
                    f = 2 * i + k
                    sp.wait_ge(u_done, 3 * NB * (f + 1))
                    sp.wait_ge(g_done, 32 * NTL * (f + 1))
                    load((f + 2) % NF1, k)
            for k in range(2):
                sp.wait_ge(in_v[k], 96 * (NF1 // 2 + 1))
                sp.wait_ge(in_s[k], 48 * (NF1 // 2 + 1))

        @block.tensor
        def _(pe):
            def second_step(f, k, unit):
                b, g = divmod(unit, 3)
                ph = 0 if g == 1 else 1
                fo = 2 if g == 0 else 0
                n = 3 * NB * f + unit
                pe.wait_ge(u_ready, n + 1)
                for part in range(2):
                    m = pe.matmul(pu[:, unit % 2, 0:2 * NF2], Ss[:, k, part, b, ph * C:ph * C + C],
                                  F[:, k, part, fo:fo + 2].rearrange("b s f -> b (s f)"),
                                  start=part == 0, stop=part == 1)
                m.then_inc(u_done, 1)

            def make_g(f, k, t):
                n = NTL * f + t
                for j in range(32):
                    pe.wait_ge(ga if j % 2 == 0 else gd, 16 * n + j // 2 + 1)
                    for e in range(4):
                        for x in range(2):
                            m = pe.matmul(pg[:, j % 4, 128 * e + 64 * x:128 * e + 64 * x + 64],
                                          AS[:, x, :, 4 * j + e],
                                          V[:, k, x, :, FT * t:FT * t + FT], start=True, stop=True)
                    m.then_inc(g_done, 1)

            def make_y(f, k, t):
                n = NTL * f + t
                if t == 0:
                    pe.wait_ge(u_ready, 3 * NB * (f + 1) + 2)
                pe.wait_ge(ga, 16 * n + 18)
                pe.wait_ge(gd, 16 * n + 18)
                for g in range(8):
                    if g % 4 == 0:
                        pe.wait_ge(ya if g == 0 else yd, n + 1)
                    for c, base in enumerate((8, 2, 6, 0)):
                        for j in range(4):
                            fr = FT * t + 4 * g + j
                            w = U[:, k, UF * fr + NB * base:UF * fr + NB * base + 32]
                            m = pe.matmul(py[32 * j:32 * j + 32, g // 4, g % 4, :], w, G[:, 4 * g + j, c, :],
                                          start=c == 0, stop=c == 3, skip_group_check=True)
                    if g % 4 == 3:
                        m.then_inc(y_done, 1)

            pe.wait_ge(in_s[0], 48)
            for unit in range(3 * NB):
                second_step(0, 0, unit)
            pe.wait_ge(as_in, 16 * 12)
            pe.wait_ge(pad_ready, 1)

            def body(f, k, i, last):
                pe.wait_ge(in_v[k], 96 * (f // 2) + 96 if isinstance(f, int) else 96 * i + 96)
                for t in range(NTL):
                    if not last:
                        if t == 0:
                            pe.wait_ge(in_s[1 - k], 48 * i + 48 + 48 * k)
                        for unit in range(3 * t, 3 * t + 3):
                            second_step(f + 1, 1 - k, unit)
                    make_g(f, k, t)
                    make_y(f, k, t)

            with pe.Fori(0, NF1 // 2) as i:
                for k in range(2):
                    body(2 * i + k, k, i, False)
            body(NF1 - 1, 0, NF1 // 2, True)

        def g_out(j):
            return G[:, :, :, 4 * j:4 * j + 4].rearrange("d f c e -> d e c f")

        def g_in(j):
            return pg[:, j % 4, :].rearrange("d (e c f) -> d e c f", e=4, c=4)

        def f_loop(eng, body):
            with eng.Fori(0, NF1 // 2) as i:
                for k in range(2):
                    body(2 * i + k, k, False)
            body(NF1 - 1, 0, True)

        @block.scalar
        def _(act):
            act.sem_inc(u_ready, 2)
            act.sem_inc(ga, 2)
            act.sem_inc(gd, 2)
            act.sem_inc(ya, 1)
            act.sem_inc(yd, 1)
            act.sem_inc(y_done, 1)
            act.sem_inc(y_out, 64)

            def u_out(f, k, unit):
                b, g = divmod(unit, 3)
                act.wait_ge(u_done, 3 * NB * f + unit + 1)
                dst = U[:, k, 0:NF2 * UF].rearrange("d (f s b) -> d b s f", s=12, b=NB)[:, b]
                src = pu[:, unit % 2, 0:2 * NF2]
                act.activation(dst[:, 2 * g], src[:, NF2:], ACT.Copy, scale=-1.0)
                act.activation(dst[:, 2 * g + 1], src[:, 0:NF2], ACT.Copy)
                act.activation(dst[:, 2 * g + 6:2 * g + 8], src.rearrange("d (s f) -> d s f", s=2),
                               ACT.Copy).then_inc(u_ready, 1)

            for unit in range(3 * NB):
                u_out(0, 0, unit)

            def body(f, k, last):
                for t in range(NTL):
                    n = NTL * f + t
                    if not last:
                        act.wait_ge(y_done, 2 * NTL * f + 1)
                        for unit in range(3 * t, 3 * t + 3):
                            u_out(f + 1, 1 - k, unit)
                    act.wait_ge(y_done, 2 * n + 1)
                    for j in range(0, 32, 2):
                        act.wait_ge(g_done, 32 * n + j + 1)
                        act.activation(g_out(j), g_in(j), ACT.Copy).then_inc(ga, 1)
                    act.wait_ge(y_out, 64 * n + 64)
                    act.wait_ge(y_done, 2 * n + 2)
                    act.activation(yo[:, 0:4, :], py[:, 0], ACT.Copy).then_inc(ya, 1)

            f_loop(act, body)

        @block.vector
        def _(v):
            v.memset(U[:, :, NF2 * UF:], 0.0).then_inc(pad_ready, 1)

            def body(f, k, last):
                for t in range(NTL):
                    n = NTL * f + t
                    v.wait_ge(y_done, 2 * n + 1)
                    for j in range(1, 32, 2):
                        v.wait_ge(g_done, 32 * n + j + 1)
                        v.tensor_copy(g_out(j), g_in(j)).then_inc(gd, 1)
                    v.wait_ge(y_out, 64 * n + 64)
                    v.wait_ge(y_done, 2 * n + 3)
                    v.tensor_copy(yo[:, 4:8, :], py[:, 1]).then_inc(yd, 1)

            f_loop(v, body)

        @block.sync
        def _(sp):
            dst = S["YD"].rearrange("f (t g j) r e -> f t j r g e", t=NTL, j=4)

            def body(f, k, last):
                for t in range(NTL):
                    n = NTL * f + t
                    sp.wait_ge(ya, n + 2)
                    sp.wait_ge(yd, n + 2)
                    for j in range(4):
                        sp.dma_start(one(dst[:, t, j], f), yo[32 * j:32 * j + 16]).then_inc(y_out, 16)

            f_loop(sp, body)
            sp.wait_ge(y_out, 64 * NF1 * NTL + 64)


def inverse(nc, I, S):
    with Arena(nc, "ivs") as A:
        Y = A.sb("y", [P, 2, 2, 2, CH])
        F = A.sb("f", [P, 2, 3, P])
        to = A.sb("to", [P, 2, 2, 2 * CH])
        pt = A.ps("pt", [P, 2, 2, 2 * CH])
        loads = [A.sem(f"loads{k}") for k in range(2)]
        t_out = [A.sem(f"t_out{k}") for k in range(2)]
        t_done, tr, ti = A.sem("t_done"), A.sem("tr"), A.sem("ti")
        block = A.ctx.enter_context(nc.Block())

        def f_loop(eng, body):
            with eng.Fori(0, NF1 // 2) as i:
                for k in range(2):
                    body(2 * i + k, k, i)
            body(NF1 - 1, 0, NF1 // 2)

        def at(ap, f):
            return ap[f] if isinstance(f, int) else ap[bass.ds(f, 1)].rearrange("o p m -> (o p) m")

        @block.gpsimd
        def _(pool):
            def body(f, k, i):
                pool.wait_ge(t_done, 2 * f + 2)
                pool.dma_start(Y[:, k].rearrange("p x c m -> p (x c m)"),
                               at(S["YD"].rearrange("f p r e -> f p (r e)"), f)).then_inc(loads[k], 16)
                pool.dma_start(F[:, k].rearrange("p s b -> p (s b)"), at(I["fi"], f)).then_inc(loads[k], 16)

            f_loop(pool, body)

        @block.tensor
        def _(pe):
            pe.sem_inc(t_done, 4)

            def body(f, k, i):
                pe.wait_ge(loads[k], 32 * i + 32)
                for c, free in ((0, tr), (1, ti)):
                    pe.wait_ge(free, f + 1)
                    for x in range(2):
                        for part, w in enumerate(((0, 2), (1, 0))[c]):
                            m = pe.matmul(pt[:, k, c, CH * x:CH * x + CH], F[:, k, w, :], Y[:, k, x, part, :],
                                          start=part == 0, stop=part == 1)
                    m.then_inc(t_done, 1)

            f_loop(pe, body)

        @block.scalar
        def _(act):
            act.sem_inc(tr, 2)
            act.sem_inc(ti, 2)
            act.sem_inc(t_out[0], 32)
            act.sem_inc(t_out[1], 32)

            def body(f, k, i):
                act.wait_ge(t_out[k], 32 * i + 32)
                act.wait_ge(t_done, 2 * f + 5)
                act.activation(to[:, k, 0, :], pt[:, k, 0, :], ACT.Copy).then_inc(tr, 1)

            f_loop(act, body)

        @block.vector
        def _(v):
            def body(f, k, i):
                v.wait_ge(t_out[k], 32 * i + 32)
                v.wait_ge(t_done, 2 * f + 6)
                v.tensor_copy(to[:, k, 1, :], pt[:, k, 1, :]).then_inc(ti, 1)

            f_loop(v, body)

        @block.sync
        def _(sp):
            def body(f, k, i):
                for c, ready in ((0, tr), (1, ti)):
                    sp.wait_ge(ready, f + 3)
                    sp.dma_start(at(S["TD"], f + 16 * c), to[:, k, c, :]).then_inc(t_out[k], 16)

            f_loop(sp, body)
            for k in range(2):
                sp.wait_ge(t_out[k], 32 * (NF1 // 2 + 1 - k) + 32)


def tokens_back(nc, I, S, X):
    HB = 32
    D = 4
    with Arena(nc, "bck") as A:
        d2 = A.sb("d2", [P, 64])
        Tt = A.sb("t", [P, D, 2 * NB * C])
        px = A.ps("px", [P, 2, 8, 64])
        const_in = A.sem("const_in")
        loads = [A.sem(f"loads{k}") for k in range(D)]
        x_done, x_added = A.sem("x_done"), A.sem("x_added")
        block = A.ctx.enter_context(nc.Block())

        @block.sync
        def _(sp):
            sp.dma_start(d2[:], S["D2M"]).then_inc(const_in, 16)
            sp.dma_start(X[:].rearrange("c (b t) -> c b t", b=NB),
                         S["X1C"].rearrange("b c t -> c b t")).then_inc(const_in, 16)

        @block.gpsimd
        def _(pool):
            src = S["TD"][0:32].rearrange("f (l h) m -> h (f l) m", l=4)
            with pool.Fori(0, HB // D) as i:
                for k in range(D):
                    pool.wait_ge(x_done, D * i + k + 1)
                    pool.dma_start(Tt[:, k], src[bass.ds(D * i + k, 1)].rearrange("o q m -> (o q) m")).then_inc(loads[k], 16)

        @block.tensor
        def _(pe):
            pe.sem_inc(x_done, D)
            pe.wait_ge(const_in, 32)
            with pe.Fori(0, HB // D) as i:
                for k in range(D):
                    pe.wait_ge(loads[k], 16 * i + 16)
                    pe.wait_ge(x_added, D * i + k + 1)
                    for n in range(8):
                        m = pe.matmul(px[:, k % 2, n, :], Tt[:, k, C * n:C * n + C], d2[:], start=True, stop=True)
                    m.then_inc(x_done, 1)

        @block.vector
        def _(v):
            v.sem_inc(x_added, 2)
            v.wait_ge(const_in, 32)
            with v.Fori(0, HB // D) as i:
                for k in range(D):
                    v.wait_ge(x_done, D * i + k + 1 + D)
                    xs = X[:].rearrange("c (b q h x) -> c h x b q", b=NB, q=64, x=2)[:, bass.ds(D * i + k, 1)].rearrange(
                        "c o x b q -> c (o x) b q")
                    v.tensor_tensor(xs, px[:, k % 2].rearrange("c (x b) q -> c x b q", x=2), xs, ALU.add).then_inc(x_added, 1)


def ln_tensor(pe, onesm, src, pm, pvar, sq, s, n, credit=0, depth=2):
    for j in range(depth):
        pe.wait_ge(s["src"], depth * n + j + 1 + credit)
        pe.wait_ge(s["d"], depth * n + j + 1)
        pe.matmul(pm[:, j], onesm[:], src(j), start=True, stop=True).then_inc(s["mean"], 1)
    for j in range(depth):
        pe.wait_ge(s["sq"], depth * n + j + 1)
        pe.wait_ge(s["sd"], depth * n + j + 1)
        pe.matmul(pvar[:, j], onesm[:], sq[:, j], start=True, stop=True).then_inc(s["var"], 1)


def ln_vector(v, src, pm, d, sd, out, s, n, depth=2):
    for j in range(depth):
        v.wait_ge(s["mean"], depth * n + j + 1)
        v.wait_ge(s["out"], depth * n + j + 1)
        v.tensor_tensor(d[:, j], src(j), pm[:, j], ALU.subtract).then_inc(s["d"], 1)
    for j in range(depth):
        v.wait_ge(s["rs"], depth * n + j + 1)
        v.tensor_tensor(out(j), d[:, j], sd[:, j], ALU.mult).then_inc(s["out"], 1)


def ln_scalar(act, d, sq, sd, pvar, eps, s, n, depth=2):
    for j in range(depth):
        act.wait_ge(s["d"], depth * n + j + 1 + depth)
        act.wait_ge(s["var"], depth * n + j + 1)
        act.activation(sq[:, j], d[:, j], ACT.Square).then_inc(s["sq"], 1)
    for j in range(depth):
        act.wait_ge(s["var"], depth * n + j + 1 + depth)
        act.wait_ge(s["out"], depth * n + j + 1)
        act.activation(sd[:, j], pvar[:, j], ACT.Ln, bias=eps[:]).then_inc(s["sd"], 1)
    for j in range(depth):
        act.wait_ge(s["sd"], depth * n + j + 1 + depth)
        act.activation(sd[:, j], sd[:, j], ACT.Exp, scale=-0.5).then_inc(s["rs"], 1)


def ln_sems(A, tag):
    return {k: A.sem(f"{tag}_{k}") for k in ("src", "mean", "d", "sq", "var", "sd", "rs", "out")}


def second_norm(nc, I, X, XN, pool4):
    NQ, D = NB * NCH, 4
    with Arena(nc, "ln2") as A:
        onesm = A.sb("onesm", [P, P])
        eps = A.sb("eps", [P, 1])
        d = A.sb("d", [P, D, CH])
        sq = A.sb("sq", [P, D, CH])
        sd = A.sb("sd", [P, D, CH])
        pm = A.ps("pm", [P, D, CH])
        pvar = A.ps("pvar", [P, D, CH])
        s = ln_sems(A, "s")
        set_up, pooled = A.sem("set_up"), A.sem("pooled")
        block = A.ctx.enter_context(nc.Block())

        def chunk(T_, i, j):
            return T_[:, bass.ds((D * i + j) * CH, CH)]

        @block.gpsimd
        def _(pool):
            pool.memset(onesm[:], 1.0 / C).then_inc(set_up, 1)
            pool.memset(eps[:], EPS_C).then_inc(set_up, 1)
            pool.sem_inc(s["src"], NQ)
            for name in ("d", "var", "sd", "out"):
                pool.sem_inc(s[name], D)

        @block.tensor
        def _(pe):
            pe.wait_ge(set_up, 2)
            with pe.Fori(0, NQ // D) as i:
                ln_tensor(pe, onesm, lambda j: chunk(X, i, j), pm, pvar, sq, s, i, depth=D)

        @block.scalar
        def _(act):
            act.wait_ge(set_up, 2)
            with act.Fori(0, NQ // D) as i:
                ln_scalar(act, d, sq, sd, pvar, eps, s, i, D)

        @block.vector
        def _(v):
            with v.Fori(0, NQ // D) as i:
                ln_vector(v, lambda j: chunk(X, i, j), pm, d, sd, lambda j: chunk(XN, i, j), s, i, D)
                for j in range(D):
                    v.wait_ge(s["out"], D * i + j + 1 + D)
                    v.tensor_reduce(pool4[:, bass.ds((D * i + j) * 32, 32)],
                                    chunk(XN, i, j).rearrange("c (r w) -> c r w", w=16), AX.X, ALU.add)


def gates(nc, I, XN, pool4, cosp, ci):
    with Arena(nc, "gat") as A:
        wsp, bsp = A.sb("wsp", [16, 9]), A.sb("bsp", [9, 1])
        wo1, bo1, wo2, bo2 = A.sb("wo1", [P, 8]), A.sb("bo1", [8, 1]), A.sb("wo2", [8, C]), A.sb("bo2", [9, C])
        wi1, bi1, wi2, bi2 = A.sb("wi1", [P, 8]), A.sb("bi1", [8, 1]), A.sb("wi2", [8, C]), A.sb("bi2", [P, 1])
        onek = A.sb("onek", [P, 1])
        p16 = A.sb("p16", [P, NB, 16])
        gap = A.sb("gap", [P, NB])
        gaps = A.sb("gaps", [P, NB])
        xs, sp_ = A.sb("xs", [16, NB]), A.sb("sp", [9, NB])
        ho, hi, hob = A.sb("ho", [8, NB]), A.sb("hi", [8, NB]), A.sb("hob", [8, NB, 9])
        ct = A.sb("ct", [9, NB, C])
        ps = A.ps("ps", [P, 512])
        pq = A.ps("pq", [P, 512])
        pr = A.ps("pr", [P, 512])
        w_in, chain, pe_done = A.sem("w_in"), A.sem("chain"), A.sem("pe_done")
        block = A.ctx.enter_context(nc.Block())

        @block.sync
        def _(sp):
            for dst, name in ((wsp, "W_sp"), (bsp, "b_sp"), (wo1, "W_o1"), (bo1, "b_o1"), (wo2, "W_o2"),
                              (wi1, "W_i1"), (bi1, "b_i1"), (wi2, "W_i2"), (bi2, "b_i2")):
                sp.dma_start(dst[:], I[name]).then_inc(w_in, 16)
            sp.dma_start(bo2[:], I["b_o2"].partition_broadcast(9)).then_inc(w_in, 16)
            sp.wait_ge(w_in, 160)

        @block.vector
        def _(v):
            n = [0]

            def step(ins):
                n[0] += 1
                ins.then_inc(chain, 1)
                v.wait_ge(chain, n[0])

            v.wait_ge(w_in, 160)
            step(v.memset(onek[:], 1.0 / (C * 256)))
            step(v.tensor_reduce(p16[:].rearrange("c b (y x) -> c (b y) x", x=4),
                                 pool4[:].rearrange("c (q r x) -> c q x r", r=16, x=4), AX.X, ALU.add))
            step(v.tensor_reduce(gaps[:], p16[:], AX.X, ALU.add))
            step(v.tensor_scalar(gap[:], gaps[:], 1.0 / T, None, ALU.mult))
            v.wait_ge(pe_done, 1)
            step(v.tensor_copy(xs[:], ps[0:16, 0:NB]))
            step(v.tensor_scalar(ho[:], ps[0:8, 8:8 + NB], bo1[:], 0.0, ALU.add, ALU.max))
            step(v.tensor_scalar(hi[:], ps[0:8, 16:16 + NB], bi1[:], 0.0, ALU.add, ALU.max))
            step(v.tensor_copy(hob[:], ho[:].rearrange("p (b o) -> p b o", o=1).to_broadcast([8, NB, 9])))
            v.wait_ge(pe_done, 2)
            step(v.tensor_scalar(sp_[:], pq[0:9, 0:NB], bsp[:], None, ALU.add))
            step(v.tensor_scalar(ci[:], pq[:, 8:8 + NB], bi2[:], None, ALU.add))
            for b in range(NB):
                step(v.tensor_tensor(ct[:, b], pr[0:9, C * b:C * b + C], bo2[:], ALU.add))
                step(v.tensor_scalar(cosp[:, b], ct[:, b], sp_[:, b:b + 1], None, ALU.mult))

        @block.tensor
        def _(pe):
            pe.wait_ge(chain, 4)
            pe.wait_ge(w_in, 160)
            for b in range(NB):
                pe.matmul(ps[0:16, b:b + 1], p16[:, b], onek[:], start=True, stop=True)
            pe.matmul(ps[0:8, 8:8 + NB], wo1[:], gap[:], start=True, stop=True)
            pe.matmul(ps[0:8, 16:16 + NB], wi1[:], gap[:], start=True, stop=True).then_inc(pe_done, 1)
            pe.wait_ge(chain, 8)
            pe.matmul(pq[0:9, 0:NB], wsp[:], xs[:], start=True, stop=True)
            pe.matmul(pq[:, 8:8 + NB], wi2[:], hi[:], start=True, stop=True)
            for b in range(NB):
                m = pe.matmul(pr[0:9, C * b:C * b + C], hob[:, b], wo2[:], start=True, stop=True)
            m.then_inc(pe_done, 1)


def image(nc, S, XN, ci):
    with Arena(nc, "img") as A:
        vr = A.sb("vr", [1, 4, CH])
        pv = A.ps("pv", [1, 4, CH])
        v_done, vr_ready = A.sem("v_done"), A.sem("vr_ready")
        v_out = [A.sem(f"v_out{k}") for k in range(4)]
        block = A.ctx.enter_context(nc.Block())

        @block.tensor
        def _(pe):
            for q in range(NB * NCH):
                if q >= 4:
                    pe.wait_ge(vr_ready, q - 3)
                pe.matmul(pv[:, q % 4], ci[:, q // NCH:q // NCH + 1], XN[:, CH * q:CH * q + CH],
                          start=True, stop=True).then_inc(v_done, 1)

        @block.scalar
        def _(act):
            for q in range(NB * NCH):
                act.wait_ge(v_done, q + 1)
                if q >= 4:
                    act.wait_ge(v_out[q % 4], 16 * (q // 4))
                act.activation(vr[:, q % 4], pv[:, q % 4], ACT.Copy).then_inc(vr_ready, 1)

        @block.sync
        def _(sp):
            for q in range(NB * NCH):
                b, n = divmod(q, NCH)
                sp.wait_ge(vr_ready, q + 1)
                sp.dma_start(S["VP"][8 * n + 1:8 * n + 9, b, 1:65], 
                             vr[:, q % 4].rearrange("o (h w) -> o h w", w=W)).then_inc(v_out[q % 4], 16)
            for k in range(4):
                sp.wait_ge(v_out[k], 16 * (NB * NCH // 4))


def experts(nc, I, S, X, cosp, out):
    GR = 2048
    NGR, GC, GT = NB * T // GR, GR // CH, GR // P
    NCHAIN = 20
    NM = NE - 2
    with Arena(nc, "moe") as A:
        ident, onesm, eps = A.sb("ident", [P, P]), A.sb("onesm", [P, P]), A.sb("eps", [P, 1])
        ew, rw = A.sb("ew", [P, NE * C]), A.sb("rw", [P, NE])
        rb, prio = A.sb("rb", [P, NE]), A.sb("prio", [P, NE])
        eb = A.sb("eb", [P, GT, C])
        v9, cs = A.sb("v9", [9, 32, W]), A.sb("cs", [9, C])
        x3 = A.sb("x3", [P, GC, CH])
        z = A.sb("z", [P, GC, CH])
        d, sq, sd = A.sb("d", [P, 2, CH]), A.sb("sq", [P, 2, CH]), A.sb("sd", [P, 2, CH])
        gb = A.sb("gb", [P, 8, GT, NE])
        g1 = A.sb("g1", [P, 8, GT])
        gt = A.sb("gt", [P, P])
        yt = A.sb("yt", [P, 3, 2, C])
        fin = A.sb("fin", [P, 2, CH])
        ex = A.ps("ex", [P, 6, CH])
        pl = A.ps("pl", [P, CH])
        pf = A.ps("pf", [P, CH])
        pm, pvar = ex[:, 0:2], ex[:, 2:4]
        const_in, set_up, v9_in = A.sem("const_in"), A.sem("set_up"), A.sem("v9_in")
        s = ln_sems(A, "s")
        cs_ready, conv_done, lg_done = A.sem("cs_ready"), A.sem("conv_done"), A.sem("lg_done")
        arg_ready, exp_ready, gate_ready = A.sem("arg_ready"), A.sem("exp_ready"), A.sem("gate_ready")
        gt_turned, gt_ready, chain = A.sem("gt_turned"), A.sem("gt_ready"), A.sem("chain")
        begun = A.sem("begun")
        mixed, yt_used, fin_ready = A.sem("mixed"), A.sem("yt_used"), A.sem("fin_ready")
        outs = [A.sem(f"outs{k}") for k in range(2)]
        block = A.ctx.enter_context(nc.Block())

        @block.sync
        def _(sp):
            for dst, src in ((ident[:], I["ident"]), (ew[:], I["expert_w"]), (rw[:], I["router_w"]),
                             (rb[:], I["router_b"].partition_broadcast(P)), (prio[:], I["prio8"])):
                sp.dma_start(dst, src).then_inc(const_in, 16)
            sp.wait_ge(set_up, 3)
            for t in range(GT):
                sp.dma_start(eb[NE * t:NE * t + NE, t, :], I["expert_b"]).then_inc(const_in, 16)
            dst = out.rearrange("b c (h n m) -> b h n c m", h=2, n=GC)
            with sp.Fori(0, NGR) as i:
                for n in range(GC):
                    sp.wait_ge(fin_ready, GC * i + n + 3)
                    sp.dma_start(dst[bass.ds(i // 2, 1), bass.ds(i % 2, 1), n].rearrange(
                        "o a c m -> (o a c) m"), fin[:, n % 2]).then_inc(outs[n % 2], 16)
            for k in range(2):
                sp.wait_ge(outs[k], 16 * NGR * GC // 2 + 16)

        @block.gpsimd
        def _(pool):
            pool.memset(eb[:], 0.0).then_inc(set_up, 1)
            pool.memset(onesm[:], 1.0 / C).then_inc(set_up, 1)
            pool.memset(eps[:], EPS_T).then_inc(set_up, 1)
            for name in ("d", "var", "sd", "out"):
                pool.sem_inc(s[name], 2)
            pool.sem_inc(s["src"], 1)
            pool.sem_inc(conv_done, GC)
            pool.sem_inc(fin_ready, 2)
            pool.sem_inc(yt_used, 2)
            pool.sem_inc(mixed, 2 * NM)
            rows = S["VP"].rearrange("h b w -> b h w")
            with pool.Fori(0, NGR) as i:
                pool.wait_ge(conv_done, GC * i + GC)
                for ti in range(3):
                    src = rows[bass.ds(i // 2, 1), bass.ds((i % 2) * 32 + ti, 32), :]
                    for tj in range(3):
                        pool.dma_start(v9[3 * ti + tj:3 * ti + tj + 1], src[:, :, tj:tj + W]).then_inc(v9_in, 16)

        @block.tensor
        def _(pe):
            def final(i, t):
                if t == 0:
                    pe.wait_ge(gt_ready, i + 1)
                if t % 4 == 0:
                    pe.wait_ge(fin_ready, GC * i + t // 4 + 2)
                pe.wait_ge(mixed, NM * (GT * i + t) + 3 * NM)
                o = pf[:, P * (t % 4):P * (t % 4) + P]
                pe.matmul(o, yt[:, t % 3, 0], ident[:], start=True, stop=False)
                pe.matmul(o, yt[:, t % 3, 1], ident[:], start=False, stop=False)
                pe.matmul(o, eb[:, t], gt[:], start=False, stop=True).then_inc(yt_used, 1)

            pe.wait_ge(const_in, 16 * (5 + GT))
            pe.wait_ge(set_up, 3)
            with pe.Fori(0, NGR) as i:
                pe.wait_ge(v9_in, 144 * i + 144)
                pe.wait_ge(cs_ready, i + 1)
                pe.wait_ge(fin_ready, GC * i + 2)
                pe.wait_ge(mixed, NM * GT * i + 2 * NM)
                for h in range(GC // 2):
                    for j in range(2):
                        n = 2 * h + j
                        pe.wait_ge(s["src"], GC * i + n + 1)
                        pe.matmul(pf[:], cs[:], v9[:, 8 * n:8 * n + 8, :].rearrange("p h w -> p (h w)"),
                                  start=True, stop=True).then_inc(conv_done, 1)
                    ln_tensor(pe, onesm, lambda j: x3[:, 2 * h + j], pm, pvar, sq, s, (GC // 2) * i + h, 1)
                pe.wait_ge(s["out"], GC * i + GC + 2)
                for t in range(GT):
                    m = pe.matmul(pl[:, NE * t:NE * t + NE], z[:, t // 4, P * (t % 4):P * (t % 4) + P], rw[:],
                                  start=True, stop=True)
                m.then_inc(lg_done, 1)
                for t in range(GT):
                    if t >= 3:
                        pe.wait_ge(mixed, NM * (GT * i + t))
                    for k in range(2):
                        m = pe.matmul(ex[:, 2 * (t % 3) + k], z[:, t // 4, P * (t % 4):P * (t % 4) + P],
                                      ew[:, CH * k:CH * k + CH], start=True, stop=True)
                    m.then_inc(lg_done, 1)
                    if t == 1:
                        pe.wait_ge(gate_ready, i + 1)
                        pe.transpose(pl[:, P:2 * P], gb[:, 7].rearrange("p t e -> p (t e)"), ident[:]).then_inc(gt_turned, 1)
                    if t >= 2:
                        final(i, t - 2)
                final(i, GT - 2)
                final(i, GT - 1)

        @block.scalar
        def _(act):
            act.sem_inc(outs[0], 16)
            act.sem_inc(outs[1], 16)
            act.wait_ge(set_up, 3)
            with act.Fori(0, NGR) as i:
                act.wait_ge(conv_done, GC * i + GC)
                act.activation(cs[:], cosp[:, bass.ds(i // 2, 1), :].rearrange("p o c -> p (o c)"), ACT.Copy).then_inc(cs_ready, 1)
                for h in range(GC // 2):
                    ln_scalar(act, d, sq, sd, pvar, eps, s, (GC // 2) * i + h)
                act.wait_ge(arg_ready, i + 1)
                act.activation(gb[:, 2], gb[:, 1], ACT.Exp).then_inc(exp_ready, 1)
                act.wait_ge(gate_ready, i + 1)
                for t in range(GT):
                    act.wait_ge(lg_done, (GT + 1) * i + t + 2)
                    act.wait_ge(yt_used, GT * i + max(t, 2))
                    for k in range(2):
                        act.activation(yt[:, t % 3, k], ex[:, 2 * (t % 3) + k, 0:C], ACT.Identity,
                                       scale=gb[:, 7, t, 4 * k:4 * k + 1]).then_inc(begun, 1)
                    if t == 0:
                        act.wait_ge(gt_turned, i + 1)
                        act.activation(gt[:], pl[:, P:2 * P], ACT.Copy).then_inc(gt_ready, 1)

        @block.vector
        def _(v):
            def bc(col):
                return g1[:, col].rearrange("p (t o) -> p t o", o=1).to_broadcast([P, GT, NE])

            def row(a):
                return a[:].rearrange("p (o e) -> p o e", o=1).to_broadcast([P, GT, NE])

            def gate(i):
                n = [0]

                def step(ins):
                    n[0] += 1
                    ins.then_inc(chain, 1)
                    v.wait_ge(chain, NCHAIN * i + n[0])

                v.wait_ge(lg_done, (GT + 1) * i + 1)
                step(v.tensor_tensor(gb[:, 0], pl[:, 0:GT * NE].rearrange("p (t e) -> p t e", e=NE), row(rb), ALU.add))
                step(v.tensor_reduce(g1[:, 0], gb[:, 0], AX.X, ALU.max))
                v.tensor_tensor(gb[:, 1], gb[:, 0], bc(0), ALU.subtract).then_inc(arg_ready, 1)
                v.wait_ge(exp_ready, i + 1)
                step(v.tensor_reduce(g1[:, 1], gb[:, 2], AX.X, ALU.add))
                step(v.reciprocal(g1[:, 2], g1[:, 1]))
                step(v.tensor_tensor(gb[:, 3], gb[:, 2], bc(2), ALU.mult))
                for r, (src, col, hot) in enumerate(((3, 3, 6), (4, 5, 5))):
                    step(v.tensor_reduce(g1[:, col], gb[:, src], AX.X, ALU.max))
                    step(v.tensor_tensor(gb[:, 5], gb[:, src], bc(col), ALU.is_equal))
                    step(v.tensor_tensor(gb[:, 5], gb[:, 5], row(prio), ALU.mult))
                    step(v.tensor_reduce(g1[:, 4], gb[:, 5], AX.X, ALU.max))
                    step(v.tensor_tensor(gb[:, hot], gb[:, 5], bc(4), ALU.is_equal))
                    if r == 0:
                        step(v.scalar_tensor_tensor(gb[:, 4], gb[:, 6], -2.0, gb[:, 3], ALU.mult, ALU.add))
                step(v.tensor_tensor(g1[:, 6], g1[:, 3], g1[:, 5], ALU.add))
                step(v.reciprocal(g1[:, 7], g1[:, 6]))
                step(v.tensor_tensor(gb[:, 6], gb[:, 6], gb[:, 5], ALU.add))
                step(v.tensor_tensor(gb[:, 6], gb[:, 6], gb[:, 3], ALU.mult))
                v.tensor_tensor(gb[:, 7], gb[:, 6], bc(7), ALU.mult).then_inc(gate_ready, 1)
                v.wait_ge(gate_ready, i + 1)
                assert n[0] == NCHAIN, n[0]

            def finish_chunk(i, n):
                v.wait_ge(yt_used, GT * i + 4 * n + 4 + 2)
                v.wait_ge(outs[n % 2], 16 * (GC // 2 * i + n // 2) + 16)
                v.tensor_tensor(fin[:, n % 2], x3[:, n], pf[:], ALU.add).then_inc(fin_ready, 1)

            with v.Fori(0, NGR) as i:
                for h in range(GC // 2):
                    for n in (2 * h, 2 * h + 1):
                        v.wait_ge(conv_done, GC * i + n + 1 + GC)
                        v.tensor_tensor(x3[:, n], X[:, bass.ds(i * GR + n * CH, CH)], pf[:], ALU.add).then_inc(s["src"], 1)
                    v.wait_ge(s["src"], GC * i + 2 * h + 3)
                    ln_vector(v, lambda j: x3[:, 2 * h + j], pm, d, sd, lambda j: z[:, 2 * h + j], s, (GC // 2) * i + h)
                gate(i)
                for t in range(GT):
                    v.wait_ge(lg_done, (GT + 1) * i + t + 2)
                    for m in range(NM):
                        k, e = m % 2, m // 2 + 1
                        src, ge = ex[:, 2 * (t % 3) + k, C * e:C * e + C], gb[:, 7, t, 4 * k + e:4 * k + e + 1]
                        if e == 1:
                            v.wait_ge(begun, 2 * (GT * i + t) + k + 1)
                        else:
                            v.wait_ge(mixed, NM * (GT * i + t) + m - 1 + 2 * NM)
                        v.scalar_tensor_tensor(yt[:, t % 3, k], src, ge, yt[:, t % 3, k],
                                               ALU.mult, ALU.add).then_inc(mixed, 1)
                    if t % 4 == 1 and t > 4:
                        finish_chunk(i, t // 4 - 1)
                finish_chunk(i, GC - 1)


def layer_one(nc, I, S, out):
    with Arena(nc, "l1") as A:
        X = A.sb("x", [P, NB * T])
        cosp, ci = A.sb("cosp", [9, NB, C]), A.sb("ci", [P, NB])
        tokens_back(nc, I, S, X)
        with Arena(nc, "l1n") as B:
            XN = B.sb("xn", [P, NB * T])
            pool4 = B.sb("pool4", [P, NB * NCH * 32])
            second_norm(nc, I, X, XN, pool4)
            gates(nc, I, XN, pool4, cosp, ci)
            image(nc, S, XN, ci)
        experts(nc, I, S, X, cosp, out)


STAGES = (prepare, normalise_in, involution, forward, filters, spectrum, inverse, layer_one)


def tables():
    a, bl = np.arange(NA), np.arange(8)
    d1 = np.zeros((NA, 8, 2, 16, 8))
    th = 2 * np.pi * np.outer(a, np.arange(17)) / 32
    for k in bl:
        d1[:, k, 0, :, k] = np.cos(th[:, 0:16])
        d1[:, k, 1, 0, k] = np.cos(th[:, 16])
        d1[:, k, 1, 1:, k] = -np.sin(th[:, 1:16])
    b, f2 = np.arange(P), np.arange(NF2)
    fw = np.zeros((NF1, P, 2, 4, NF2))
    fi = np.zeros((NF1, NF2, 3, P))
    for f1 in range(NF1):
        f = f1 + 32 * f2
        for z in range(2):
            t = 2 * np.pi * (np.outer(b + z, f) % 4096) / 4096
            c, s = np.cos(t), np.sin(t)
            fw[f1, :, 0, 2 * z:2 * z + 2] = np.stack([c, -s], 1)
            if f1 not in (0, 16):
                fw[f1, :, 1, 2 * z:2 * z + 2] = np.stack([s, c], 1)
        t = 2 * np.pi * (np.outer(f, b) % 4096) / 4096
        w = (1.0 if f1 in (0, 16) else 2.0) / 4096
        fi[f1] = np.stack([np.cos(t), np.sin(t), -np.sin(t)], 1) * w
    d2 = np.zeros((32, 4, NA, 4))
    for k in range(4):
        d2[0:17, k, :, k] = np.cos(2 * np.pi * np.outer(np.arange(17), a) / 32)
        d2[17:, k, :, k] = -np.sin(2 * np.pi * np.outer(np.arange(1, 16), a) / 32)
    return {
        "ident": np.eye(P), "d1": d1.reshape(P, 2 * P), "fw": fw.reshape(NF1, P, 8 * NF2),
        "fi": fi.reshape(NF1, NF2, 3 * P), "d2": d2.reshape(P, 64), 
        "prio": np.tile(np.array([4.0, 3.0, 2.0, 1.0]), (P, 1)),
        "prio8": np.tile(np.arange(8.0, 0.0, -1.0), (P, 1)),
    }


def delta():
    d = np.zeros((T, 2), np.float32)
    d[0:2, 0] = 1.0
    d[2, 1] = 1.0
    return d


def layout(a):
    g = np.ascontiguousarray
    r = {
        "x": a["x"].reshape(NB, C, T), "w_reduce": a["L0_conv_w_reduce"], "b_reduce": a["L0_conv_b_reduce"].reshape(-1, 1),
        "w_span": a["L0_conv_w_span"].reshape(NG, TAPS, 32).transpose(2, 1, 0).reshape(32, -1),
        "b_span": a["L0_conv_b_span"].reshape(NG, TAPS).T.reshape(1, -1),
        "sigma": a["L0_ffn_sigma"], "phix": np.concatenate([a["L0_ffn_phi"], delta()], 1), "Mu": a["L0_ffn_M_u"], "Mpp": a["L0_ffn_M_phi_plus"],
        "Mpm": a["L0_ffn_M_phi_minus"], "lw": a["L0_ffn_log_weights"], "gum": a["L0_ffn_gumbel"],
        "W_sp": a["L1_conv_W_sp"], "b_sp": a["L1_conv_b_sp"].reshape(-1, 1), "W_o1": a["L1_conv_W_o1"],
        "b_o1": a["L1_conv_b_o1"].reshape(-1, 1), "W_o2": a["L1_conv_W_o2"], "b_o2": a["L1_conv_b_o2"],
        "W_i1": a["L1_conv_W_i1"], "b_i1": a["L1_conv_b_i1"].reshape(-1, 1), "W_i2": a["L1_conv_W_i2"],
        "b_i2": a["L1_conv_b_i2"].reshape(-1, 1), "router_w": a["L1_ffn_router_w"], "router_b": a["L1_ffn_router_b"],
        "expert_w": a["L1_ffn_expert_w"].transpose(1, 0, 2).reshape(C, NE * C), "expert_b": a["L1_ffn_expert_b"],
    }
    return {k: g(v) for k, v in r.items()}


def build(nc, I, out, stages):
    def dram(name, shape, dt=F32):
        return nc.dram_tensor(name, shape, dt).ap()

    S = {
        "XN": dram("s_xn", [NB, H, WP, C]), "XT": dram("s_xt", [NB * T, C]),
        "XNC": dram("s_xnc", [NB * NCH, C, CH]), "X1": dram("s_x1", [NB * T, C]),
        "X1C": dram("s_x1c", [NB, C, T]), "SF": dram("s_sf", [NB, 33, P, 2 * C]), "SP": dram("s_sp", [33, P, 2 * KX]),
        "WC": dram("s_wc", [P, TAPS * NG]), "KB": dram("s_kb", [1, TAPS * NG]), "D2M": dram("s_d2m", [P, 64]),
        "AS": dram("s_as", [2, 3, KX, C, C], BF16), "VP": dram("s_vp", [66, NB, 66]),
        "VS": dram("s_vs", [3, NF1, KX, 2, 2, NF2], BF16),
        "YD": dram("s_yd", [NF1, NF2, 16, C]), "TD": dram("s_td", [33, P, 2 * NB * C]),
    }
    for f in stages:
        f(nc, I, S, out) if f is layer_one else f(nc, I, S)


def kernel(**inputs):
    import concourse.bacc as bacc
    from concourse.bass_utils import run_bass_kernel_spmd

    nc = bacc.Bacc("TRN2", target_bir_lowering=False, num_devices=1)
    arrays, I = {}, {}
    for name, a in layout({k: np.asarray(v) for k, v in inputs.items()}).items():
        arrays[f"in_{name}"] = a
        I[name] = nc.dram_tensor(f"in_{name}", a.shape, mybir.dt.from_np(a.dtype), kind="ExternalInput").ap()
    for name, a in tables().items():
        a = a.astype(np.float32)
        arrays[f"table_{name}"] = a
        I[name] = nc.dram_tensor(f"table_{name}", a.shape, F32, kind="ExternalInput").ap()
    out = nc.dram_tensor("out", (NB, C, T), F32, kind="ExternalOutput").ap()
    build(nc, I, out, STAGES)
    r = run_bass_kernel_spmd(nc, [arrays], core_ids=[0])
    return r.results[0]["out"].reshape(NB, C, H, W)
```
